# Optimizing a Trainium2 kernel written in Bass

```python
import numpy as np
import jax
import jax.numpy as jnp

def _softmax(x, axis=-1):
    return jax.nn.softmax(x, axis=axis)

def _gelu(x):
    return jax.nn.gelu(x, approximate=True)

def _silu(x):
    return jax.nn.silu(x)

def _sigmoid(x):
    return jax.nn.sigmoid(x)

def _layernorm(x, axis=-1, eps=1e-05):
    m = jnp.mean(x, axis=axis, keepdims=True)
    v = jnp.var(x, axis=axis, keepdims=True)
    return (x - m) / jnp.sqrt(v + eps)

def _scatter_add(tgt, idx, src, axis=0):
    return tgt.at[idx].add(src)

def _segment_sum(src, seg, n):
    return jax.ops.segment_sum(src, seg, n)
kernel_name = 'mk_vit_tower_postln_d1_tok_img768_r4_d61e68'

def setup_inputs(seed: int=0):
    np.random.seed(seed)
    _w = jnp.asarray

    def _rec_inputs():
        import jax
        import jax.numpy as jnp
        _rk = jax.random.key(seed)
        x = -0.000356955 + 1 * jax.random.normal(jax.random.fold_in(_rk, 1), (64, 224, 224, 3), jnp.float32)
        return x
    x = _rec_inputs()

    def _L0_tok_setup():
        import jax, jax.numpy as jnp
        import numpy as np
        PATCH = 16
        IMG = 224
        NP_SIDE = IMG // PATCH
        EMBED = 192

        def _patchify(batch_image):
            B = batch_image.shape[0]
            x = batch_image.reshape(B, NP_SIDE, PATCH, NP_SIDE, PATCH, 3)
            x = x.transpose(0, 1, 3, 5, 2, 4)
            return x.reshape(B, NP_SIDE * NP_SIDE, 3 * PATCH * PATCH)
        key = jax.random.key(seed)
        k1, k2, k3, k4, k5 = jax.random.split(key, 5)
        return {'batch_image': jax.random.normal(k1, (128, IMG, IMG, 3), dtype=jnp.float32), 'W': jax.random.normal(k2, (EMBED, 3 * PATCH * PATCH), dtype=jnp.float32) * 0.02, 'b': jax.random.normal(k3, (EMBED,), dtype=jnp.float32) * 0.02, 'cls_token': jax.random.normal(k4, (1, 1, EMBED), dtype=jnp.float32), 'pos_embed': jax.random.normal(k5, (1, NP_SIDE * NP_SIDE + 1, EMBED), dtype=jnp.float32)}
    _L0_tok_all = _L0_tok_setup()
    _L0_tok_in = {k: v for k, v in _L0_tok_all.items() if k in ('W', 'b', 'cls_token', 'pos_embed')}
    del _L0_tok_all

    def _L0_attn_setup():
        import jax, jax.numpy as jnp
        import numpy as np
        D_MODEL, D_STATE, D_CONV, D_INNER = (192, 16, 4, 384)
        B, L = (4, 1024)

        def _mamba_fwd(x, w_in, w_conv, w_xproj, w_dt, b_dt, a_log, d_param, w_out):
            Lseq = x.shape[1]
            xz = x @ w_in.T
            xs, z = jnp.split(xz, 2, axis=-1)
            xc = xs.transpose(0, 2, 1)
            xc = jax.lax.conv_general_dilated(xc, w_conv, window_strides=(1,), padding=[(D_CONV - 1, 0)], feature_group_count=D_INNER, dimension_numbers=('NCH', 'OIH', 'NCH'))
            xs = jax.nn.silu(xc.transpose(0, 2, 1))
            proj = xs @ w_xproj.T
            delta_raw = proj[..., :1]
            b_proj = proj[..., 1:1 + D_STATE]
            c_proj = proj[..., 1 + D_STATE:]
            delta = jax.nn.softplus(delta_raw @ w_dt.T + b_dt)
            a_mat = -jnp.exp(a_log)

            def step(h, inp):
                dt, bt, ct, xt = inp
                a_bar = jnp.exp(dt[:, :, None] * a_mat)
                h = a_bar * h + dt[:, :, None] * bt[:, None, :] * xt[:, :, None]
                y = jnp.einsum('bn,bdn->bd', ct, h) + d_param * xt
                return (h, y)
            h0 = jnp.zeros((x.shape[0], D_INNER, D_STATE), x.dtype)
            inputs = (delta.transpose(1, 0, 2), b_proj.transpose(1, 0, 2), c_proj.transpose(1, 0, 2), xs.transpose(1, 0, 2))
            _, ys = jax.lax.scan(step, h0, inputs, length=Lseq)
            y = ys.transpose(1, 0, 2)
            return y * jax.nn.silu(z) @ w_out.T
        key = jax.random.key(seed)
        ks = jax.random.split(key, 9)
        s = 0.02
        return {'x': jax.random.normal(ks[0], (B, L, D_MODEL), jnp.float32), 'w_in': jax.random.normal(ks[1], (2 * D_INNER, D_MODEL), jnp.float32) * s, 'w_conv': jax.random.normal(ks[2], (D_INNER, 1, D_CONV), jnp.float32) * 0.2, 'w_xproj': jax.random.normal(ks[3], (2 * D_STATE + 1, D_INNER), jnp.float32) * s, 'w_dt': jax.random.normal(ks[4], (D_INNER, 1), jnp.float32) * s, 'b_dt': jax.random.normal(ks[5], (D_INNER,), jnp.float32) * 0.1, 'a_log': jnp.log(jnp.tile(jnp.arange(1, D_STATE + 1, dtype=jnp.float32), (D_INNER, 1))), 'd_param': jnp.ones((D_INNER,), jnp.float32), 'w_out': jax.random.normal(ks[6], (D_MODEL, D_INNER), jnp.float32) * s}
    _L0_attn_all = _L0_attn_setup()
    _L0_attn_in = {k: v for k, v in _L0_attn_all.items() if k in ('w_in', 'w_conv', 'w_xproj', 'w_dt', 'b_dt', 'a_log', 'd_param', 'w_out')}
    del _L0_attn_all

    def _L0_ffn_setup():
        import jax, jax.numpy as jnp
        import numpy as np
        B_SZ, S, D = (8, 128, 192)
        H = 12
        N_EXP = 8
        RANK = 16
        ALPHA = 32
        TOP_K = 2
        key = jax.random.key(seed)
        ks = jax.random.split(key, 9)
        x = jax.random.normal(ks[0], (B_SZ, S, D), jnp.float32)
        W_qkv = jax.random.normal(ks[1], (3 * D, D), jnp.float32) * 0.02
        b_qkv = jnp.zeros((3 * D,), jnp.float32)
        W_gate = jax.random.normal(ks[2], (N_EXP, D), jnp.float32) * 0.02
        b_gate = jnp.zeros((N_EXP,), jnp.float32)
        A = jax.random.normal(ks[3], (N_EXP, RANK, D), jnp.float32) * 0.02
        B_lora = jax.random.normal(ks[4], (N_EXP, 3 * D, RANK), jnp.float32) * 0.02
        W_proj = jax.random.normal(ks[5], (D, D), jnp.float32) * 0.02
        b_proj = jnp.zeros((D,), jnp.float32)
        return {'x': x, 'W_qkv': W_qkv, 'b_qkv': b_qkv, 'W_gate': W_gate, 'b_gate': b_gate, 'A': A, 'B_lora': B_lora, 'W_proj': W_proj, 'b_proj': b_proj}
    _L0_ffn_all = _L0_ffn_setup()
    _L0_ffn_in = {k: v for k, v in _L0_ffn_all.items() if k in ('W_qkv', 'b_qkv', 'W_gate', 'b_gate', 'A', 'B_lora', 'W_proj', 'b_proj')}
    del _L0_ffn_all
    return {'x': x, 'L0_tok_W': _L0_tok_in['W'], 'L0_tok_b': _L0_tok_in['b'], 'L0_tok_cls_token': _L0_tok_in['cls_token'], 'L0_tok_pos_embed': _L0_tok_in['pos_embed'], 'L0_attn_w_in': _L0_attn_in['w_in'], 'L0_attn_w_conv': _L0_attn_in['w_conv'], 'L0_attn_w_xproj': _L0_attn_in['w_xproj'], 'L0_attn_w_dt': _L0_attn_in['w_dt'], 'L0_attn_b_dt': _L0_attn_in['b_dt'], 'L0_attn_a_log': _L0_attn_in['a_log'], 'L0_attn_d_param': _L0_attn_in['d_param'], 'L0_attn_w_out': _L0_attn_in['w_out'], 'L0_ffn_W_qkv': _L0_ffn_in['W_qkv'], 'L0_ffn_b_qkv': _L0_ffn_in['b_qkv'], 'L0_ffn_W_gate': _L0_ffn_in['W_gate'], 'L0_ffn_b_gate': _L0_ffn_in['b_gate'], 'L0_ffn_A': _L0_ffn_in['A'], 'L0_ffn_B_lora': _L0_ffn_in['B_lora'], 'L0_ffn_W_proj': _L0_ffn_in['W_proj'], 'L0_ffn_b_proj': _L0_ffn_in['b_proj']}

def reference(x, L0_tok_W, L0_tok_b, L0_tok_cls_token, L0_tok_pos_embed, L0_attn_w_in, L0_attn_w_conv, L0_attn_w_xproj, L0_attn_w_dt, L0_attn_b_dt, L0_attn_a_log, L0_attn_d_param, L0_attn_w_out, L0_ffn_W_qkv, L0_ffn_b_qkv, L0_ffn_W_gate, L0_ffn_b_gate, L0_ffn_A, L0_ffn_B_lora, L0_ffn_W_proj, L0_ffn_b_proj):
    import jax
    import jax.numpy as jnp

    def _L0_tok_ref(batch_image, W, b, cls_token, pos_embed):
        import jax, jax.numpy as jnp
        import numpy as np
        PATCH = 16
        IMG = 224
        NP_SIDE = IMG // PATCH
        EMBED = 192

        def _patchify(batch_image):
            B = batch_image.shape[0]
            x = batch_image.reshape(B, NP_SIDE, PATCH, NP_SIDE, PATCH, 3)
            x = x.transpose(0, 1, 3, 5, 2, 4)
            return x.reshape(B, NP_SIDE * NP_SIDE, 3 * PATCH * PATCH)
        B = batch_image.shape[0]
        patches = _patchify(batch_image)
        Zp = jnp.einsum('bpd,ed->bpe', patches, W) + b
        Zcls = jnp.broadcast_to(cls_token, (B, 1, EMBED))
        Zcls_p = jnp.concatenate([Zcls, Zp], axis=1)
        return Zcls_p + pos_embed

    def _L0_attn_ref(x, w_in, w_conv, w_xproj, w_dt, b_dt, a_log, d_param, w_out):
        import jax, jax.numpy as jnp
        import numpy as np
        D_MODEL, D_STATE, D_CONV, D_INNER = (192, 16, 4, 384)
        B, L = (4, 1024)

        def _mamba_fwd(x, w_in, w_conv, w_xproj, w_dt, b_dt, a_log, d_param, w_out):
            Lseq = x.shape[1]
            xz = x @ w_in.T
            xs, z = jnp.split(xz, 2, axis=-1)
            xc = xs.transpose(0, 2, 1)
            xc = jax.lax.conv_general_dilated(xc, w_conv, window_strides=(1,), padding=[(D_CONV - 1, 0)], feature_group_count=D_INNER, dimension_numbers=('NCH', 'OIH', 'NCH'))
            xs = jax.nn.silu(xc.transpose(0, 2, 1))
            proj = xs @ w_xproj.T
            delta_raw = proj[..., :1]
            b_proj = proj[..., 1:1 + D_STATE]
            c_proj = proj[..., 1 + D_STATE:]
            delta = jax.nn.softplus(delta_raw @ w_dt.T + b_dt)
            a_mat = -jnp.exp(a_log)

            def step(h, inp):
                dt, bt, ct, xt = inp
                a_bar = jnp.exp(dt[:, :, None] * a_mat)
                h = a_bar * h + dt[:, :, None] * bt[:, None, :] * xt[:, :, None]
                y = jnp.einsum('bn,bdn->bd', ct, h) + d_param * xt
                return (h, y)
            h0 = jnp.zeros((x.shape[0], D_INNER, D_STATE), x.dtype)
            inputs = (delta.transpose(1, 0, 2), b_proj.transpose(1, 0, 2), c_proj.transpose(1, 0, 2), xs.transpose(1, 0, 2))
            _, ys = jax.lax.scan(step, h0, inputs, length=Lseq)
            y = ys.transpose(1, 0, 2)
            return y * jax.nn.silu(z) @ w_out.T
        return _mamba_fwd(x, w_in, w_conv, w_xproj, w_dt, b_dt, a_log, d_param, w_out)

    def _L0_ffn_ref(x, W_qkv, b_qkv, W_gate, b_gate, A, B_lora, W_proj, b_proj):
        import jax, jax.numpy as jnp
        import numpy as np
        B_SZ, S, D = (8, 128, 192)
        H = 12
        N_EXP = 8
        RANK = 16
        ALPHA = 32
        TOP_K = 2
        b, s, d = x.shape
        n_exp, rank = (A.shape[0], A.shape[1])
        scaling = ALPHA / rank
        head_dim = d // H
        scale = head_dim ** (-0.5)
        t = b * s
        x_flat = x.reshape(t, d)
        qkv_base = x @ W_qkv.T + b_qkv
        logits = x_flat @ W_gate.T + b_gate
        router_probs = jax.nn.softmax(logits, axis=-1)
        top_k_weights, top_k_indices = jax.lax.top_k(router_probs, TOP_K)
        a_down = jnp.einsum('td,nrd->tnr', x_flat, A)
        expert_out = jnp.einsum('tnr,nor->tno', a_down, B_lora) * scaling
        dispatch = jnp.zeros((t, n_exp), x.dtype).at[jnp.arange(t)[:, None], top_k_indices].add(top_k_weights)
        sparse_out = jnp.einsum('tno,tn->to', expert_out, dispatch)
        qkv = qkv_base + sparse_out.reshape(b, s, 3 * d)
        qkv = qkv.reshape(b, s, 3, H, head_dim).transpose(2, 0, 3, 1, 4)
        q, k, v = (qkv[0], qkv[1], qkv[2])
        attn = jax.nn.softmax(jnp.einsum('bhqd,bhkd->bhqk', q, k) * scale, axis=-1)
        out = jnp.einsum('bhqk,bhkd->bhqd', attn, v)
        out = out.transpose(0, 2, 1, 3).reshape(b, s, d)
        return out @ W_proj.T + b_proj
    h = _L0_tok_ref(x, L0_tok_W, L0_tok_b, L0_tok_cls_token, L0_tok_pos_embed)
    h = _layernorm(h + _L0_attn_ref(h, L0_attn_w_in, L0_attn_w_conv, L0_attn_w_xproj, L0_attn_w_dt, L0_attn_b_dt, L0_attn_a_log, L0_attn_d_param, L0_attn_w_out), axis=-1)
    h = _layernorm(h + _L0_ffn_ref(h, L0_ffn_W_qkv, L0_ffn_b_qkv, L0_ffn_W_gate, L0_ffn_b_gate, L0_ffn_A, L0_ffn_B_lora, L0_ffn_W_proj, L0_ffn_b_proj), axis=-1)
    return h

_drawn_inputs = setup_inputs


def setup_inputs(seed=0):
    import zlib

    import numpy as np

    out = dict(_drawn_inputs(seed))
    spreads = {'L0_attn_d_param': (1.0, 0.6),
     'L0_ffn_b_qkv': (0.0, 0.324),
     'L0_ffn_b_gate': (0.0, 0.8),
     'L0_ffn_b_proj': (0.0, 0.1)}
    factors = {'L0_tok_b': 3.209,
     'L0_attn_w_in': 8.0,
     'L0_attn_w_conv': 8.0,
     'L0_attn_w_xproj': 8.0,
     'L0_attn_w_dt': 8.0,
     'L0_attn_b_dt': 8.0,
     'L0_attn_a_log': 8.0,
     'L0_attn_w_out': 8.0,
     'L0_ffn_W_qkv': 8.0,
     'L0_ffn_W_gate': 8.0,
     'L0_ffn_A': 8.0,
     'L0_ffn_B_lora': 8.0}
    for name, (base, spread) in spreads.items():
        noise = np.random.default_rng([zlib.crc32(name.encode()), seed]).standard_normal(out[name].shape)
        drawn = base * np.exp(spread * noise) if base else spread * noise
        out[name] = jnp.asarray(drawn.astype(out[name].dtype))
    for name, factor in factors.items():
        out[name] = (out[name] * factor).astype(out[name].dtype)
    return out
```

```python
import concourse.bass as bass
from concourse import mybir
from contextlib import ExitStack

NB, SIDE, PATCH, CH = 64, 14, 16, 3
EMB, DIN, NST, NTAP = 192, 384, 16, 4
NEXP, RANK, ALPHA = 8, 16, 32
HEADS, HD = 12, 16
LTOK = SIDE * SIDE + 1
NPATCH = SIDE * SIDE
G = 2
NPAIR = NB // G
T = G * LTOK
TP = G * NPATCH
KP = CH * PATCH * PATCH // 128
DC = DIN // 128
ROWS = (LTOK + 1) // 2
NTILE = 2 * G
HSLOT = 32
HPC = 128 // HSLOT
HC = HEADS // HPC
QPC = 6
QC = HEADS // QPC
MROW = QPC * HD
PADW = 256
SCALE = float(HD) ** -0.5
EPS = 1e-5
LN_EXP_TABLES, SILU_TABLES = 6, 18


class Pair:

    def __init__(self, j, off):
        self.j, self.off = j, off

    def plus(self, d):
        return Pair(self.j, self.off + d)

    @property
    def parity(self):
        return self.off % 2

    def has(self, d):
        return self.j is not None or self.off + d >= 0

    def times(self, k, c):
        v = self.off * k + c
        return v if self.j is None else self.j * (2 * k) + v


class Order:

    def __init__(self, names):
        self.names = list(names)
        self.at = {n: k for k, n in enumerate(self.names)}
        assert len(self.at) == len(self.names)
        self.n = 0

    def step(self, name):
        assert self.names[self.n % len(self.names)] == name, (name, self.names[self.n % len(self.names)])
        self.n += 1
        return 1

    def count(self, pair, name):
        return pair.times(len(self.names), self.at[name] + 1)


def tower_kernel(nc, x, w_patch, pos, cls, b_patch, w_in, w_conv, w_proj_bc, w_proj_dt, w_dt, b_dt,
                 a_log, d_param, w_out, w_qk, w_v, w_gate, w_down, w_o, res0, res1, resb,
                 ident, swap, sel, kmask, vmask, rev, out):
    fp32, bf16 = mybir.dt.float32, mybir.dt.bfloat16
    ALU = mybir.AluOpType
    ACT = mybir.ActivationFunctionType
    AX = mybir.AxisListType

    ctx = ExitStack()
    with ctx:
        def sb(name, shape, dt=fp32):
            return ctx.enter_context(nc.sbuf_tensor(name, shape, dt))

        def sem(name):
            return ctx.enter_context(nc.semaphore(name))

        wpatch_sb = sb("wpatch_sb", [128, KP, EMB])
        pos_sb = [sb("pos0_sb", [128, LTOK]), sb("pos1_sb", [64, LTOK])]
        cls_sb = sb("cls_sb", [128, 2])
        bp_sb = sb("bp_sb", [128, 2])
        win_sb = sb("win_sb", [128, 2, 2 * DIN])
        conv_sb = sb("conv_sb", [128, DC, NTAP])
        wbc_sb = sb("wbc_sb", [128, DC, 96])
        wraw_sb = sb("wraw_sb", [128, DC, 1])
        wdt_sb = sb("wdt_sb", [128, DC])
        bdt_sb = sb("bdt_sb", [128, DC])
        negA = sb("negA", [128, DC, NST])
        d_sb = sb("d_sb", [128, DC])
        wout_sb = sb("wout_sb", [128, DC, EMB])
        wqk_sb = sb("wqk_sb", [128, 3, 2 * QC * 128])
        wv_sb = sb("wv_sb", [128, 3, EMB])
        wgate_sb = sb("wgate_sb", [128, 2, NEXP])
        wdown_sb = sb("wdown_sb", [128, 2, 128])
        wo_sb = sb("wo_sb", [128, HC, EMB])
        res0_sb = sb("res0_sb", [128, EMB])
        res1_sb = sb("res1_sb", [128, EMB])
        resb_sb = sb("resb_sb", [128, EMB])
        id_sb = sb("id_sb", [128, 128])
        swap_sb = sb("swap_sb", [128, 128])
        sel_sb = sb("sel_sb", [96, 2 * NST, 128], bf16)
        kmask_sb = sb("kmask_sb", [128, QPC])
        vmask_sb = sb("vmask_sb", [ROWS, 1])
        rev_sb = sb("rev_sb", [ROWS, NTILE, NEXP])

        xin = sb("xin", [128, KP, TP])
        hT = [[sb(f"hT{m}_{b}", [128, G, LTOK]) for m in range(2)] for b in range(2)]
        xpad = sb("xpad", [128, DC, G, LTOK + 3])
        cv = sb("cv", [128, DC, T])
        ex = sb("ex", [128, DC, T])
        xs = [sb(f"xs{b}", [128, DC, T]) for b in range(2)]
        sz = [sb(f"sz{b}", [128, DC, T]) for b in range(2)]
        dt = [sb(f"dt{b}", [128, DC, T]) for b in range(2)]
        dtx = [sb(f"dtx{b}", [128, DC, T]) for b in range(2)]
        bc = [sb(f"bc{b}", [96, T], bf16) for b in range(2)]
        bcrest = sb("bcrest", [64, T])
        NA, NU = 2, 4
        abar = [sb(f"abar{k}", [128, DC, G, LTOK]) for k in range(NA)]
        state = [sb(f"state{k}", [128, DC, T]) for k in range(NU)]
        yacc = sb("yacc", [128, DC, T])
        y = sb("y", [128, DC, T])
        st = sb("st", [ROWS, NTILE, 6])
        mv = sb("mv", [ROWS, NTILE, 2])
        rs = sb("rs", [ROWS, NTILE])
        h1 = sb("h1", [ROWS, NTILE, PADW])
        h1T = [sb(f"h1T{m}", [128, T]) for m in range(2)]
        gk = [sb(f"gk{k}", [ROWS, NTILE, NEXP]) for k in range(5)]
        gs = sb("gs", [ROWS, NTILE])
        ad = sb("ad", [128, T])
        aw = sb("aw", [128, T])
        km = sb("km", [128, HEADS, T])
        q = sb("q", [128, QC, T])
        va = sb("va", [ROWS, NTILE, HEADS, HSLOT])
        mpad = sb("mpad", [ROWS, NTILE, QC * 128])
        pT = [sb(f"pT{k}", [ROWS, 2, HPC, LTOK]) for k in range(2)]
        wrank = pT[0][:].rearrange("p k h t -> p (k h t)")[:, 0:NTILE * 128]
        o = sb("o", [128, HC, T])
        rinv = y
        fin = h1[:, :, 0:EMB]
        eps_sb = sb("eps_sb", [ROWS, 1])

        PS = ctx.enter_context(nc.psum_tensor("PS", [128, 8, 512], fp32))
        BB, CB, AB, FB = 0, 2, 4, 7
        NBC, NAB = 2, 3

        s_load = sem("s_load")
        s_cast = sem("s_cast")
        s_setup = sem("s_setup")
        s_setup2 = sem("s_setup2")
        s_x = sem("s_x")
        s_apart = sem("s_apart")
        s_out = sem("s_out")

        steps = range(NST)
        front_pe = sem("front_pe")
        f_pe = Order(["patch0", "patch1"] + [f"xz{m}" for m in range(6)] + ["raw", "bc"])
        front_act = sem("front_act")
        f_act = Order([f"xz{m}" for m in range(6)] + ["xs", "sz"]
                      + [f"abs{c}" for c in range(DC)] + [f"relu{c}" for c in range(DC)] + ["ep", "lp"])
        SMALL = 2.0 ** -6
        front_dve = sem("front_dve")
        f_dve = Order(["hT0", "hT1"] + [f"conv{c}{j}" for c in range(DC) for j in range(NTAP)]
                      + ["series"]
                      + [f"split{k}" for k in range(5)] + ["large", "chosen"])
        front_pool = sem("front_pool")
        f_pool = Order(["series", "small", "dt", "dtx"])
        b_broadcast = sem("b_broadcast")
        b_done = Order(steps)
        c_broadcast = sem("c_broadcast")
        c_done = Order(steps)
        state_summed = sem("state_summed")
        n_done = Order(steps)
        skip_term = sem("skip_term")
        k_done = Order(range(DC))
        input_term = sem("input_term")
        u_done = Order(steps)
        scanned = sem("scanned")
        h_done = Order(steps)
        c_applied = sem("c_applied")
        hc_done = Order(steps)
        decayed = sem("decayed")
        a_done = Order(steps)

        groups = [(g, j) for g in range(G) for j in range(HC)]
        smax = [(g, qt, hp) for g in range(G) for qt in range(2) for hp in range(HEADS // 2)]
        uses = [("out0", "d", "norm1"), ("out1", "d", "norm3"), ("h1T0", "a", "h1T0"), ("h1T1", "a", "h1T1"),
                ("gate", "d", "gd"), ("down", "a", "down"), ("spread", "d", "aw"),
                ("v0", "a", "v1"), ("v1", "a", "v3")]
        for j in range(QC):
            uses += [(f"k{j}", "a", f"k{j}{QPC - 1}"), (f"q{j}", "a", f"q{j}")]
        uses += [(f"s{k}", "d", f"max{k}") for k in range(len(smax))]
        uses += [(f"m{j}", "d", f"qm{j}") for j in range(QC)]
        seq = []
        for k in range(len(groups) + 1):
            if k < len(groups):
                seq += [("t", k, kt, hp) for kt in range(2) for hp in range(2)]
            if k >= 1:
                seq += [("pv", k - 1)]
        for s in seq:
            uses.append(("t%d%d%d" % s[1:], "a", "e%d%d%d" % s[1:]) if s[0] == "t" else (f"pv{s[1]}", "a", f"o{s[1]}"))
        uses += [(f"r{j}", "a", f"lr{j}") for j in range(HC)] + [("proj0", "d", "fin1"), ("proj1", "d", "fin3")]
        turn = {u[0]: k for k, u in enumerate(uses)}

        gated = sem("gated")
        z_done = Order(["yz"])
        attn_pe = sem("attn_pe")
        a_pe = Order([u[0] for u in uses])
        attn_act = sem("attn_act")
        a_act = Order(["ln0", "ln1", "h1T0", "h1T1", "ge", "down"]
                      + [f"v{t}" for t in range(NTILE)]
                      + [n for j in range(QC) for n in [f"k{j}{i}" for i in range(QPC)] + [f"q{j}"]]
                      + [("e%d%d%d" % s[1:]) if s[0] == "t" else f"o{s[1]}" for s in seq]
                      + [f"lr{j}" for j in range(HC)] + ["er", "ln2", "ln3"])
        attn_dve = sem("attn_dve")
        a_dve = Order([f"st{t}" for t in range(NTILE)] + [f"mv{t}" for t in range(NTILE)]
                      + [f"norm{t}" for t in range(NTILE)]
                      + ["gmx", "gd", "gs", "gr", "gp"]
                      + [f"{a}0" for a in ("gm", "ge", "gc", "gt", "go")] + ["gx"]
                      + [f"{a}1" for a in ("gm", "ge", "gc", "gt", "go")] + ["gu", "gw", "gwr", "aw"]
                      + [f"max{k}" for k in range(len(smax))] + [f"qm{j}" for j in range(QC)]
                      + ["on"] + [f"ft{t}" for t in range(NTILE)] + [f"fv{t}" for t in range(NTILE)]
                      + [f"fin{t}" for t in range(NTILE)])

        def apart(engine):
            engine.sem_inc(s_apart, 1)

        def bank(name):
            return AB + turn[name] % NAB

        def last_read(p, name):
            k = turn[name] - NAB
            if k < 0:
                if not p.has(-1):
                    return attn_act, None
                k = max(i for i in range(len(uses)) if i % NAB == turn[name] % NAB)
                p = p.plus(-1)
            _, who, what = uses[k]
            return (attn_act, a_act.count(p, what)) if who == "a" else (attn_dve, a_dve.count(p, what))

        def cols(tile):
            g, qt = tile // 2, tile % 2
            a = g * LTOK + qt * (LTOK - ROWS)
            return slice(a, a + ROWS)

        def flat(t):
            return t[:, :, :].rearrange("p c t -> p (c t)")

        def tok(h):
            return h[:, :, :].rearrange("p g t -> p (g t)")

        score_plan = [f"s{k}" for k in range(len(smax))]
        value_plan = [("t%d%d%d" % s[1:]) if s[0] == "t" else f"pv{s[1]}" for s in seq]

        FRONT = {"patch", "xz", "conv", "silu", "raw", "series", "bc", "log", "chosen"}
        TAIL = {"proj", "fin"}
        pe_plan = {0: ["patch0", "proj"], 1: ["out0", "out1"], 2: ["patch1", "h1T"], 3: ["gate", "xz0", "xz1"],
                   4: ["spread", "v", "k0"], 5: ["q0", "k1", "q1", "xz2"],
                   6: ["xz3"] + score_plan[:6] + ["xz4"], 7: score_plan[6:14] + ["xz5"], 8: score_plan[14:22],
                   9: score_plan[22:] + ["raw", "m"] + value_plan[:2],
                   10: value_plan[2:8], 11: ["bc"] + value_plan[8:14], 12: value_plan[14:20], 13: value_plan[20:26],
                   14: value_plan[26:], 15: ["r"]}
        act_plan = {1: ["fin"], 2: ["norm"], 3: ["h1T", "xz0"], 4: ["gate", "xz1", "v", "k0"],
                    5: ["q0", "k1", "q1", "xz2"], 6: ["xz3", "xz4"], 7: ["xz5"], 8: ["silu"],
                    9: ["raw"] + value_plan[:2], 10: value_plan[2:8], 11: value_plan[8:14], 12: ["log"] + value_plan[14:20],
                    13: value_plan[20:26], 14: value_plan[26:], 15: ["r"]}
        dve_plan = {0: ["yz"], 1.6: ["fin"], 2.6: ["patch0", "norm"], 3: ["patch1"], 4: ["gate", "conv0"], 4.6: ["aw"],
                    5.3: ["conv1"], 6.6: ["conv2"] + score_plan[:6], 7.6: score_plan[6:14], 8.6: score_plan[14:22],
                    9.6: score_plan[22:] + ["m"], 10.6: ["series"], 11.6: ["bc"], 13: ["chosen"], 15.6: ["r"]}
        pool_plan = {11: ["series"], 13: ["chosen"]}

        def works(plan, n, f, a, z):
            for w in plan.get(n, []):
                p = z if w in TAIL else f if w.rstrip("0123456789") in FRONT else a
                if p:
                    yield w, p

        def program(engine, loop, part):
            def it(j, i, f=True, s=True, a=True, z=True):
                part(Pair(j, i + 1) if f else None, Pair(j, i) if s else None,
                     Pair(j, i - 1) if a else None, Pair(j, i - 2) if z else None)

            it(None, -1, s=False, a=False, z=False)
            it(None, 0, a=False, z=False)
            it(None, 1, z=False)
            it(None, 2)
            with engine.Fori(1, (NPAIR - 2) // 2) as j:
                it(j, 1)
                it(j, 2)
            it(None, NPAIR - 1, f=False)
            it(None, NPAIR, f=False, s=False)
            it(None, NPAIR + 1, f=False, s=False, a=False)

        NLOADS = 31
        block = ctx.enter_context(nc.Block())

        @block.sync
        def _(sp):
            loads = [(wpatch_sb[:], w_patch), (pos_sb[0][:], pos[0:128, :]), (pos_sb[1][:], pos[128:EMB, :]),
                     (cls_sb[:], cls), (bp_sb[:], b_patch), (win_sb[:], w_in), (conv_sb[:], w_conv),
                     (wbc_sb[:], w_proj_bc), (wraw_sb[:], w_proj_dt), (wdt_sb[:], w_dt), (bdt_sb[:], b_dt),
                     (negA[:], a_log), (d_sb[:], d_param), (wout_sb[:], w_out), (wqk_sb[:], w_qk),
                     (wv_sb[:], w_v), (wgate_sb[:], w_gate), (wdown_sb[:], w_down), (wo_sb[:], w_o),
                     (res0_sb[:], res0), (res1_sb[:], res1), (resb_sb[:], resb), (id_sb[:], ident),
                     (swap_sb[:], swap), (kmask_sb[:], kmask), (vmask_sb[:], vmask), (rev_sb[:], rev),
                     (state[0][0:96, :, :].rearrange("p c t -> p (c t)")[:, 0:1024], sel[:, 0:1024]),
                     (state[1][0:96, :, :].rearrange("p c t -> p (c t)")[:, 0:1024], sel[:, 1024:2048]),
                     (state[2][0:96, :, :].rearrange("p c t -> p (c t)")[:, 0:1024], sel[:, 2048:3072]),
                     (state[3][0:96, :, :].rearrange("p c t -> p (c t)")[:, 0:1024], sel[:, 3072:4096])]
            assert len(loads) == NLOADS
            for dst, src in loads:
                sp.dma_start(dst, src).then_inc(s_load, 16)

            def part(f, s, a, z):
                if f:
                    if f.has(-1):
                        sp.wait_ge(front_pe, f_pe.count(f.plus(-1), "patch1"))
                    src = x[f.off] if f.j is None else x[f.j * 2 + f.off]
                    sp.dma_start(xin[:], src).then_inc(s_x, 16)
                if z:
                    sp.wait_ge(attn_dve, a_dve.count(z, "fin3"))
                    dst = out[z.off] if z.j is None else out[z.j * 2 + z.off]
                    sp.dma_start(dst[:, 0:ROWS, :].rearrange("g t e -> t g e"),
                                 fin[:, 0:NTILE:2, :]).then_inc(s_out, 16)
                    sp.dma_start(dst[:, ROWS:LTOK, :].rearrange("g t e -> t g e"),
                                 fin[1:ROWS, 1:NTILE:2, :]).then_inc(s_out, 16)

            program(sp, None, part)
            sp.wait_ge(s_out, 32 * NPAIR)

        @block.gpsimd
        def _(pool):
            pool.wait_ge(s_setup2, 2)

            def add_state(p, n):
                if n == 0:
                    pool.wait_ge(skip_term, k_done.count(p, DC - 1))
                else:
                    pool.wait_ge(state_summed, n_done.count(p, n - 1))
                pool.wait_ge(c_applied, hc_done.count(p, n))
                nc.gpsimd.tensor_tensor(flat(yacc), flat(yacc), flat(state[n % NU]),
                                        ALU.add).then_inc(state_summed, n_done.step(n))

            def front(f, what):
                b = f.parity
                if what == "series":
                    pool.wait_ge(front_dve, f_dve.count(f, "series"))
                    apart(pool)
                    nc.gpsimd.tensor_scalar(flat(dtx[b]), flat(dtx[b]), 1.0 / 3, 1.0, ALU.mult,
                                            ALU.add).then_inc(front_pool, f_pool.step("series"))
                    pool.wait_ge(front_pool, f_pool.count(f, "series"))
                    if f.has(-2):
                        pool.wait_ge(decayed, a_done.count(f.plus(-2), NST - 1))
                    nc.gpsimd.tensor_tensor(flat(dt[b]), flat(dtx[b]), flat(ex),
                                            ALU.mult).then_inc(front_pool, f_pool.step("small"))
                if what == "chosen":
                    pool.wait_ge(front_dve, f_dve.count(f, "chosen"))
                    nc.gpsimd.tensor_tensor(flat(dt[b]), flat(dt[b]), flat(cv),
                                            ALU.add).then_inc(front_pool, f_pool.step("dt"))
                    pool.wait_ge(front_pool, f_pool.count(f, "dt"))
                    nc.gpsimd.tensor_tensor(flat(dtx[b]), flat(dt[b]), flat(xs[b]),
                                            ALU.mult).then_inc(front_pool, f_pool.step("dtx"))

            def part(f, s, a, z):
                for n in steps:
                    if s and n >= 1:
                        add_state(s, n - 1)
                    for w, p in works(pool_plan, n, f, a, z):
                        front(p, w)
                if s:
                    add_state(s, NST - 1)

            program(pool, None, part)

        @block.scalar
        def _(act):
            act.wait_ge(s_load, 16 * NLOADS)

            def tables(number):
                nc.scalar.add_instruction(mybir.InstLoadActFuncSet(
                    name=nc.get_next_instruction_name(), engine=mybir.EngineType.Activation,
                    act_func_set_id=number, ins=[], outs=[]))

            tables(LN_EXP_TABLES)
            nc.scalar.activation(negA[:], negA[:], ACT.Exp).then_inc(s_cast, 1)

            def decay(p, n):
                if n == 0:
                    act.wait_ge(front_pool, f_pool.count(p, "dt"))
                if n >= NA:
                    act.wait_ge(scanned, h_done.count(p, n - NA))
                else:
                    if p.has(-1):
                        act.wait_ge(scanned, h_done.count(p.plus(-1), NST + n - NA))
                b = p.parity
                for c in range(DC):
                    last = nc.scalar.activation(
                        abar[n % NA][:, c, :, 1:], dt[b][:, c, :].rearrange("p (g t) -> p g t", g=G)[:, :, 1:],
                        ACT.Exp, scale=negA[:, c, n:n + 1])
                last.then_inc(decayed, a_done.step(n))

            def skip(p):
                if p.has(-1):
                    act.wait_ge(gated, z_done.count(p.plus(-1), "yz"))
                for c in range(DC):
                    nc.scalar.activation(yacc[:, c, :], xs[p.parity][:, c, :], ACT.Copy,
                                         scale=d_sb[:, c:c + 1]).then_inc(skip_term, k_done.step(c))

            def front(f, what):
                fbank = PS[:, FB, 0:T]
                if what[:2] == "xz":
                    m = int(what[2])
                    act.wait_ge(front_pe, f_pe.count(f, what))
                    if m < DC:
                        if f.has(-1):
                            act.wait_ge(front_dve, f_dve.count(f.plus(-1), f"conv{DC - 1}{NTAP - 1}"))
                        nc.scalar.activation(xpad[:, m, :, 3:], fbank.rearrange("p (g t) -> p g t", g=G),
                                                        ACT.Copy).then_inc(front_act, f_act.step(what))
                    else:
                        if f.has(-2):
                            act.wait_ge(gated, z_done.count(f.plus(-2), "yz"))
                        nc.scalar.activation(sz[f.parity][:, m - DC, :], fbank, ACT.Copy).then_inc(front_act, f_act.step(what))
                if what == "silu":
                    b = f.parity
                    tables(SILU_TABLES)
                    act.wait_ge(front_dve, f_dve.count(f, f"conv{DC - 1}{NTAP - 1}"))
                    if f.has(-2):
                        act.wait_ge(skip_term, k_done.count(f.plus(-2), DC - 1))
                    act.wait_ge(front_act, f_act.count(f, "xz5"))
                    nc.scalar.activation(flat(xs[b]), flat(cv), ACT.Silu).then_inc(front_act, f_act.step("xs"))
                    nc.scalar.activation(flat(sz[b]), flat(sz[b]), ACT.Silu).then_inc(front_act, f_act.step("sz"))
                    tables(LN_EXP_TABLES)
                if what == "raw":
                    act.wait_ge(front_pe, f_pe.count(f, "raw"))
                    act.wait_ge(front_act, f_act.count(f, "xs"))
                    if f.has(-1):
                        act.wait_ge(front_pool, f_pool.count(f.plus(-1), "dtx"))
                    for c in range(DC):
                        nc.scalar.activation(ex[:, c, :], fbank, ACT.Abs, scale=wdt_sb[:, c:c + 1],
                                                        bias=bdt_sb[:, c:c + 1]).then_inc(front_act, f_act.step(f"abs{c}"))
                    for c in range(DC):
                        nc.scalar.activation(cv[:, c, :], fbank, ACT.Relu, scale=wdt_sb[:, c:c + 1],
                                                        bias=bdt_sb[:, c:c + 1]).then_inc(front_act, f_act.step(f"relu{c}"))
                    act.wait_ge(front_act, f_act.count(f, f"abs{DC - 1}"))
                    nc.scalar.activation(flat(ex), flat(ex), ACT.Exp, scale=-1.0).then_inc(front_act, f_act.step("ep"))
                if what == "log":
                    act.wait_ge(front_pool, f_pool.count(f, "small"))
                    nc.scalar.activation(flat(dtx[f.parity]), flat(ex), ACT.Ln, bias=1.0).then_inc(front_act, f_act.step("lp"))

            def attn(a, what):
                if what in ("norm", "fin"):
                    act.wait_ge(attn_dve, a_dve.count(a, f"mv{NTILE - 1}" if what == "norm" else f"fv{NTILE - 1}"))
                    n0, n1 = ("ln0", "ln1") if what == "norm" else ("ln2", "ln3")
                    nc.scalar.activation(rs[:], mv[:, :, 1], ACT.Ln, bias=eps_sb[:]).then_inc(attn_act, a_act.step(n0))
                    act.wait_ge(attn_act, a_act.count(a, n0))
                    nc.scalar.activation(rs[:], rs[:], ACT.Exp, scale=-0.5).then_inc(attn_act, a_act.step(n1))
                if what == "h1T":
                    for m in range(2):
                        act.wait_ge(attn_pe, a_pe.count(a, f"h1T{m}"))
                        if m == 0:
                            if a.has(-1):
                                act.wait_ge(attn_pe, a_pe.count(a.plus(-1), "proj1"))
                        nc.scalar.activation(h1T[m][:], PS[:, bank(f"h1T{m}"), 0:T], ACT.Copy).then_inc(attn_act, a_act.step(f"h1T{m}"))
                if what == "gate":
                    act.wait_ge(attn_dve, a_dve.count(a, "gd"))
                    nc.scalar.activation(gk[0][:], gk[0][:], ACT.Exp).then_inc(attn_act, a_act.step("ge"))
                    act.wait_ge(attn_pe, a_pe.count(a, "down"))
                    nc.scalar.activation(ad[:], PS[:, bank("down"), 0:T], ACT.Copy).then_inc(attn_act, a_act.step("down"))
                if what == "v":
                    for t in range(NTILE):
                        if t % 2 == 0:
                            act.wait_ge(attn_pe, a_pe.count(a, f"v{t // 2}"))
                        src = PS[0:ROWS, bank(f"v{t // 2}"), (t % 2) * EMB:(t % 2 + 1) * EMB]
                        nc.scalar.activation(va[:, t, :, 0:HD], src.rearrange("p (h d) -> p h d", d=HD),
                                                        ACT.Copy, scale=vmask_sb[:] if t % 2 else 1.0).then_inc(attn_act, a_act.step(f"v{t}"))
                if what[0] == "k" and len(what) == 2:
                    j = int(what[1])
                    act.wait_ge(attn_pe, a_pe.count(a, what))
                    for i in range(QPC):
                        nc.scalar.activation(km[:, j * QPC + i, :], PS[:, bank(what), 0:T], ACT.Copy,
                                                        scale=kmask_sb[:, i:i + 1]).then_inc(attn_act, a_act.step(f"k{j}{i}"))
                if what[0] == "q" and len(what) == 2:
                    j = int(what[1])
                    act.wait_ge(attn_pe, a_pe.count(a, what))
                    nc.scalar.activation(q[:, j, :], PS[:, bank(what), 0:T], ACT.Copy).then_inc(attn_act, a_act.step(what))
                if what[0] == "t":
                    k, kt, hp = (int(c) for c in what[1:])
                    act.wait_ge(attn_pe, a_pe.count(a, what))
                    if k >= 2:
                        act.wait_ge(attn_pe, a_pe.count(a, f"pv{k - 2}"))
                    else:
                        if a.has(-1):
                            act.wait_ge(attn_pe, a_pe.count(a.plus(-1), f"pv{len(groups) + k - 2}"))
                    nc.scalar.activation(
                        pT[k % 2][:, kt, 2 * hp:2 * hp + 2, :].rearrange("p h t -> p (h t)"),
                        PS[0:ROWS, bank(what), 0:T], ACT.Exp, scale=SCALE).then_inc(attn_act, a_act.step("e" + what[1:]))
                if what[:2] == "pv":
                    k = int(what[2])
                    g, j = groups[k]
                    act.wait_ge(attn_pe, a_pe.count(a, what))
                    if k == 0:
                        if a.has(-1):
                            act.wait_ge(attn_pe, a_pe.count(a.plus(-1), "proj1"))
                    nc.scalar.activation(o[:, j, g * LTOK:(g + 1) * LTOK], PS[:, bank(what), 0:LTOK],
                                                    ACT.Copy).then_inc(attn_act, a_act.step(f"o{k}"))
                if what == "r":
                    for j in range(HC):
                        act.wait_ge(attn_pe, a_pe.count(a, f"r{j}"))
                        nc.scalar.activation(rinv[:, j, :], PS[:, bank(f"r{j}"), 0:T], ACT.Ln).then_inc(attn_act, a_act.step(f"lr{j}"))
                    act.wait_ge(attn_act, a_act.count(a, f"lr{HC - 1}"))
                    nc.scalar.activation(flat(rinv), flat(rinv), ACT.Exp, scale=-1.0).then_inc(attn_act, a_act.step("er"))

            act.wait_ge(s_setup2, 2)

            def part(f, s, a, z):
                if s:
                    decay(s, 0)
                for n in steps:
                    if s and n + 1 < NST:
                        decay(s, n + 1)
                    if s and n == 1:
                        skip(s)
                    for w, p in works(act_plan, n, f, a, z):
                        (front if p is f else attn)(p, w)

            program(act, None, part)

        @block.vector
        def _(dve):
            TT, TS, STT = nc.vector.tensor_tensor, nc.vector.tensor_scalar, nc.vector.scalar_tensor_tensor
            nc.vector.memset(eps_sb[:], EPS).then_inc(s_setup2, 1)
            for b in range(2):
                nc.vector.memset(hT[b][1][64:128, :, :], 1.0)
            nc.vector.memset(xpad[:], 0.0)
            for k in range(NA):
                nc.vector.memset(abar[k][:], 0.0)
            nc.vector.memset(mpad[:], 0.0)
            nc.vector.memset(h1[:], 0.0)
            nc.vector.memset(va[:], 1.0).then_inc(s_setup, 1)
            dve.wait_ge(s_setup, 1)
            nc.vector.memset(va[0:1, 1:NTILE:2, :, :], 0.0)
            nc.vector.memset(h1[:, :, EMB:EMB + 1], 1.0).then_inc(s_setup, 1)
            dve.wait_ge(s_load, 16 * NLOADS)
            for m, rows in ((0, 128), (1, 64)):
                for b in range(2):
                    last = TT(hT[b][m][0:rows, :, 0], cls_sb[0:rows, m:m + 1].to_broadcast([rows, G]),
                              pos_sb[m][:, 0:1].to_broadcast([rows, G]), ALU.add)
                last = TS(pos_sb[m][:, 1:], pos_sb[m][:, 1:], bp_sb[0:rows, m:m + 1], None, ALU.add)
            for k in range(4):
                last = nc.vector.tensor_copy(
                    sel_sb[:, 8 * k:8 * k + 8, :].rearrange("p a b -> p (a b)"),
                    state[k][0:96, :, :].rearrange("p c t -> p (c t)")[:, 0:1024])
            dve.wait_ge(s_cast, 1)
            TS(negA[:], negA[:], -1.0, None, ALU.mult).then_inc(s_setup2, 1)
            dve.wait_ge(s_setup2, 2)
            dve.wait_ge(s_setup, 2)

            def term(p, n):
                if n == 0:
                    dve.wait_ge(front_pool, f_pool.count(p, "dtx"))
                dve.wait_ge(b_broadcast, b_done.count(p, n))
                if n >= NU:
                    dve.wait_ge(state_summed, n_done.count(p, n - NU))
                else:
                    if p.has(-1):
                        dve.wait_ge(state_summed, n_done.count(p.plus(-1), NST + n - NU))
                bb = PS[:, BB + n % NBC:BB + n % NBC + 1, 0:T].to_broadcast([128, DC, T])
                TT(state[n % NU][:], dtx[p.parity][:], bb, ALU.mult).then_inc(input_term, u_done.step(n))

            def times_c(p, n):
                dve.wait_ge(c_broadcast, c_done.count(p, n))
                dve.wait_ge(scanned, h_done.count(p, n))
                cb = PS[:, CB + n % NBC:CB + n % NBC + 1, 0:T].to_broadcast([128, DC, T])
                TT(state[n % NU][:], state[n % NU][:], cb, ALU.mult).then_inc(c_applied, hc_done.step(n))

            def scan(p, n):
                dve.wait_ge(decayed, a_done.count(p, n))
                dve.wait_ge(input_term, u_done.count(p, n))
                nc.vector.tensor_tensor_scan(
                    flat(state[n % NU]), abar[n % NA][:].rearrange("p c g t -> p (c g t)"), flat(state[n % NU]),
                    0.0, ALU.mult, ALU.add).then_inc(scanned, h_done.step(n))

            def front(f, what):
                b = f.parity
                if what[:5] == "patch":
                    m = int(what[5])
                    rows = (128, 64)[m]
                    dve.wait_ge(front_pe, f_pe.count(f, what))
                    if f.has(-2):
                        dve.wait_ge(attn_pe, a_pe.count(f.plus(-2), "out1"))
                    TT(hT[b][m][0:rows, :, 1:], PS[0:rows, FB, 0:TP].rearrange("p (g t) -> p g t", g=G),
                                  pos_sb[m][:, 1:].rearrange("p (o t) -> p o t", o=1).to_broadcast([rows, G, NPATCH]),
                                  ALU.add).then_inc(front_dve, f_dve.step(f"hT{m}"))
                if what[:4] == "conv":
                    c = int(what[4])
                    dve.wait_ge(front_act, f_act.count(f, f"xz{c}"))
                    if c == 0:
                        if f.has(-1):
                            dve.wait_ge(front_pool, f_pool.count(f.plus(-1), "dt"))
                    acc = cv[:, c, :].rearrange("p (g t) -> p g t", g=G)
                    TS(acc, xpad[:, c, :, 0:LTOK], conv_sb[:, c, 0:1], None, ALU.mult).then_inc(front_dve, f_dve.step(f"conv{c}0"))
                    for j in range(1, NTAP):
                        dve.wait_ge(front_dve, f_dve.count(f, f"conv{c}{j - 1}"))
                        STT(acc, xpad[:, c, :, j:j + LTOK], conv_sb[:, c, j:j + 1], acc,
                                       ALU.mult, ALU.add).then_inc(front_dve, f_dve.step(f"conv{c}{j}"))
                if what == "bc":
                    ps = PS[0:96, FB, 0:T]
                    dve.wait_ge(front_pe, f_pe.count(f, "bc"))
                    nc.vector.tensor_copy(bc[b][:], ps).then_inc(front_dve, f_dve.step("split0"))
                    dve.wait_ge(front_dve, f_dve.count(f, "split0"))
                    TT(bcrest[:], ps[0:64], bc[b][0:64, :], ALU.subtract).then_inc(front_dve, f_dve.step("split1"))
                    dve.wait_ge(front_dve, f_dve.count(f, "split1"))
                    nc.vector.tensor_copy(bc[b][0:64, :], bcrest[:]).then_inc(front_dve, f_dve.step("split2"))
                    dve.wait_ge(front_dve, f_dve.count(f, "split2"))
                    TT(bcrest[0:32, :], bcrest[0:32, :], bc[b][0:32, :], ALU.subtract).then_inc(front_dve, f_dve.step("split3"))
                    dve.wait_ge(front_dve, f_dve.count(f, "split3"))
                    nc.vector.tensor_copy(bc[b][0:32, :], bcrest[0:32, :]).then_inc(front_dve, f_dve.step("split4"))

                if what == "series":
                    dve.wait_ge(front_act, f_act.count(f, "ep"))
                    if f.has(-2):
                        dve.wait_ge(input_term, u_done.count(f.plus(-2), NST - 1))
                    STT(flat(dtx[b]), flat(ex), -1.5, flat(ex), ALU.add, ALU.mult).then_inc(front_dve, f_dve.step("series"))
                if what == "chosen":
                    dve.wait_ge(front_act, f_act.count(f, "lp"))
                    TS(flat(ex), flat(ex), -SMALL, 0.0, ALU.add, ALU.max).then_inc(front_dve, f_dve.step("large"))
                    dve.wait_ge(front_dve, f_dve.count(f, "large"))
                    apart(dve)
                    nc.vector.copy_predicated(flat(dt[b]), flat(ex).bitcast(mybir.dt.uint32), flat(dtx[b])).then_inc(front_dve, f_dve.step("chosen"))

            def attn(a, what):
                b = a.parity
                V = nc.vector

                def norm(names, source, dest):
                    s, m, w, ready, act_name = names
                    for t in range(NTILE):
                        if t % 2 == 0:
                            dve.wait_ge(attn_pe, a_pe.count(a, f"{ready}{t // 2}"))
                        V.bn_stats(st[:, t, :], source(t)).then_inc(attn_dve, a_dve.step(f"{s}{t}"))
                    dve.wait_ge(attn_dve, a_dve.count(a, f"{s}{NTILE - 1}"))
                    apart(dve)
                    for t in range(NTILE):
                        V.bn_aggr(mv[:, t, :], st[:, t, :]).then_inc(attn_dve, a_dve.step(f"{m}{t}"))
                    dve.wait_ge(attn_act, a_act.count(a, act_name))
                    for t in range(NTILE):
                        dve.wait_ge(attn_dve, a_dve.count(a, f"{m}{t}"))
                        TS(dest(t), source(t), mv[:, t, 0:1], rs[:, t:t + 1], ALU.subtract, ALU.mult).then_inc(attn_dve, a_dve.step(f"{w}{t}"))

                if what == "yz":
                    dve.wait_ge(state_summed, n_done.count(a, NST - 1))
                    if a.has(-1):
                        dve.wait_ge(attn_dve, a_dve.count(a.plus(-1), "on"))
                    TT(flat(y), flat(yacc), flat(sz[b]), ALU.mult).then_inc(gated, z_done.step("yz"))
                if what == "norm":
                    if a.j is not None or a.off > 0:
                        dve.wait_ge(s_out, a.times(32, 0))
                    norm(("st", "mv", "norm", "out", "ln1"),
                         lambda t: PS[0:ROWS, bank(f"out{t // 2}"), (t % 2) * EMB:(t % 2 + 1) * EMB],
                         lambda t: h1[:, t, 0:EMB])
                if what == "gate":
                    lg = PS[0:ROWS, bank("gate"), 0:NTILE * NEXP].rearrange("p (t n) -> p t n", n=NEXP)

                    def wide(v):
                        return v[:].rearrange("p (t o) -> p t o", o=1).to_broadcast([ROWS, NTILE, NEXP])

                    e, pr, cand, oh1, rest = (t[:] for t in gk)
                    dve.wait_ge(attn_pe, a_pe.count(a, "gate"))
                    V.reduce_max(gs[:], lg, AX.X).then_inc(attn_dve, a_dve.step("gmx"))
                    dve.wait_ge(attn_dve, a_dve.count(a, "gmx"))
                    TT(e, lg, wide(gs), ALU.subtract).then_inc(attn_dve, a_dve.step("gd"))
                    dve.wait_ge(attn_act, a_act.count(a, "ge"))
                    V.reduce_sum(gs[:], e, AX.X).then_inc(attn_dve, a_dve.step("gs"))
                    dve.wait_ge(attn_dve, a_dve.count(a, "gs"))
                    V.reciprocal(gs[:], gs[:]).then_inc(attn_dve, a_dve.step("gr"))
                    dve.wait_ge(attn_dve, a_dve.count(a, "gr"))
                    TT(pr, e, wide(gs), ALU.mult).then_inc(attn_dve, a_dve.step("gp"))
                    for k, (src, mark) in enumerate(((pr, "gp"), (rest, "gx"))):
                        dve.wait_ge(attn_dve, a_dve.count(a, mark))
                        V.reduce_max(gs[:], src, AX.X).then_inc(attn_dve, a_dve.step(f"gm{k}"))
                        dve.wait_ge(attn_dve, a_dve.count(a, f"gm{k}"))
                        TT(cand, src, wide(gs), ALU.is_ge).then_inc(attn_dve, a_dve.step(f"ge{k}"))
                        dve.wait_ge(attn_dve, a_dve.count(a, f"ge{k}"))
                        TT(cand, cand, rev_sb[:], ALU.mult).then_inc(attn_dve, a_dve.step(f"gc{k}"))
                        dve.wait_ge(attn_dve, a_dve.count(a, f"gc{k}"))
                        V.reduce_max(gs[:], cand, AX.X).then_inc(attn_dve, a_dve.step(f"gt{k}"))
                        dve.wait_ge(attn_dve, a_dve.count(a, f"gt{k}"))
                        TT(oh1 if k == 0 else cand, cand, wide(gs), ALU.is_equal).then_inc(attn_dve, a_dve.step(f"go{k}"))
                        dve.wait_ge(attn_dve, a_dve.count(a, f"go{k}"))
                        if k == 0:
                            STT(rest, oh1, -2.0, pr, ALU.mult, ALU.add).then_inc(attn_dve, a_dve.step("gx"))
                    TT(oh1, oh1, cand, ALU.add).then_inc(attn_dve, a_dve.step("gu"))
                    dve.wait_ge(attn_dve, a_dve.count(a, "gu"))
                    STT(cand, oh1, float(ALPHA) / RANK, pr, ALU.mult, ALU.mult).then_inc(attn_dve, a_dve.step("gw"))
                    dve.wait_ge(attn_dve, a_dve.count(a, "gw"))
                    wr = wrank.rearrange("p (n r) -> p n r", r=RANK)
                    V.tensor_copy(wr, cand.rearrange("p t (n o) -> p (t n) o", o=1).to_broadcast(
                        [ROWS, NTILE * NEXP, RANK])).then_inc(attn_dve, a_dve.step("gwr"))
                if what == "aw":
                    dve.wait_ge(attn_pe, a_pe.count(a, "spread"))
                    dve.wait_ge(attn_act, a_act.count(a, "down"))
                    TT(aw[:], ad[:], PS[:, bank("spread"), 0:T], ALU.mult).then_inc(attn_dve, a_dve.step("aw"))
                if what[0] == "s" and what[1:].isdigit():
                    k = int(what[1:])
                    g, qt, hp = smax[k]
                    j, i = 2 * hp // QPC, 2 * hp % QPC
                    dve.wait_ge(attn_pe, a_pe.count(a, what))
                    V.reduce_max(
                        mpad[:, 2 * g + qt, 128 * j + MROW + i:128 * j + MROW + i + 2],
                        PS[0:ROWS, bank(what), 0:T].rearrange("p (h t) -> p h t", h=2), AX.X).then_inc(attn_dve, a_dve.step(f"max{k}"))
                if what == "m":
                    for j in range(QC):
                        dve.wait_ge(attn_pe, a_pe.count(a, f"m{j}"))
                        dve.wait_ge(attn_act, a_act.count(a, f"q{j}"))
                        TT(q[:, j, :], q[:, j, :], PS[:, bank(f"m{j}"), 0:T], ALU.add).then_inc(attn_dve, a_dve.step(f"qm{j}"))
                if what == "r":
                    dve.wait_ge(attn_act, a_act.count(a, "er"))
                    TT(flat(o), flat(o), flat(rinv), ALU.mult).then_inc(attn_dve, a_dve.step("on"))
                if what == "fin":
                    norm(("ft", "fv", "fin", "proj", "ln3"),
                         lambda t: PS[0:ROWS, bank(f"proj{t // 2}"), (t % 2) * EMB:(t % 2 + 1) * EMB],
                         lambda t: fin[:, t, :])

            def part(f, s, a, z):
                if s:
                    term(s, 0)
                for n in steps:
                    if s and n + 1 < NST:
                        term(s, n + 1)
                    for w, p in works(dve_plan, n, f, a, z):
                        (front if p is f else attn)(p, w)
                    if s and n >= 1:
                        times_c(s, n - 1)
                    for w, p in works(dve_plan, n + 0.3, f, a, z):
                        (front if p is f else attn)(p, w)
                    if s:
                        scan(s, n)
                    for w, p in works(dve_plan, n + 0.6, f, a, z):
                        (front if p is f else attn)(p, w)
                if s:
                    times_c(s, NST - 1)

            program(dve, None, part)

        @block.tensor
        def _(pe):
            MM = nc.tensor.matmul
            pe.wait_ge(s_setup2, 2)
            pe.wait_ge(s_setup, 2)

            def b_row(p, n):
                if n == 0:
                    pe.wait_ge(front_dve, f_dve.count(p, "split4"))
                if n >= NBC:
                    pe.wait_ge(input_term, u_done.count(p, n - NBC))
                elif p.has(-1):
                    pe.wait_ge(input_term, u_done.count(p.plus(-1), NST + n - NBC))
                MM(PS[:, BB + n % NBC, 0:T], sel_sb[:, n, :], bc[p.parity][:],
                   start=True, stop=True).then_inc(b_broadcast, b_done.step(n))

            def c_row(p, n):
                if n >= NBC:
                    pe.wait_ge(c_applied, hc_done.count(p, n - NBC))
                elif p.has(-1):
                    pe.wait_ge(c_applied, hc_done.count(p.plus(-1), NST + n - NBC))
                MM(PS[:, CB + n % NBC, 0:T], sel_sb[:, NST + n, :], bc[p.parity][:],
                   start=True, stop=True).then_inc(c_broadcast, c_done.step(n))

            def front(f, what):
                b = f.parity
                if what == "patch0":
                    pe.wait_ge(s_x, f.times(16, 16))
                    if f.has(-1):
                        pe.wait_ge(front_dve, f_dve.count(f.plus(-1), "split1"))
                if what == "patch1":
                    pe.wait_ge(front_dve, f_dve.count(f, "hT0"))
                if what[:5] == "patch":
                    m = int(what[5])
                    rows = (128, 64)[m]
                    for k in range(KP):
                        last = MM(PS[0:rows, FB, 0:TP], wpatch_sb[:, k, 128 * m:128 * m + rows], xin[:, k, :],
                                  start=(k == 0), stop=(k == KP - 1))
                    last.then_inc(front_pe, f_pe.step(what))
                if what[:2] == "xz":
                    m = int(what[2])
                    if m == 0:
                        pe.wait_ge(front_dve, f_dve.count(f, "hT1"))
                    else:
                        pe.wait_ge(front_act, f_act.count(f, f"xz{m - 1}"))
                    MM(PS[:, FB, 0:T], win_sb[:, 0, 128 * m:128 * m + 128], tok(hT[b][0]), start=True, stop=False)
                    MM(PS[:, FB, 0:T], win_sb[0:65, 1, 128 * m:128 * m + 128], tok(hT[b][1])[0:65, :],
                                 start=False, stop=True).then_inc(front_pe, f_pe.step(what))
                if what in ("raw", "bc"):
                    pe.wait_ge(front_act, f_act.count(f, "xs" if what == "raw" else f"relu{DC - 1}"))
                    rows = 128 if what == "raw" else 96
                    for c in range(DC):
                        w = wraw_sb[:, c, :].to_broadcast([128, 128]) if what == "raw" else wbc_sb[:, c, :]
                        last = MM(PS[0:rows, FB, 0:T], w, xs[b][:, c, :], start=(c == 0), stop=(c == DC - 1))
                    last.then_inc(front_pe, f_pe.step(what))

            def attn(a, what):
                b = a.parity
                if what[:3] == "out" or what == "proj":
                    for k in ((int(what[3]),) if what != "proj" else (0, 1)):
                        name = f"{what[:3]}{k}" if what != "proj" else f"proj{k}"
                        reader, count = last_read(a, name)
                        if count is not None:
                            pe.wait_ge(reader, count)
                        if what == "proj":
                            pe.wait_ge(attn_dve, a_dve.count(a, "on"))
                            pairs = [(lambda c, j=j: o[:, j, c], wo_sb[:, j, :]) for j in range(HC)]
                            pairs += [(lambda c: h1T[0][:, c], res0_sb[:]), (lambda c: h1T[1][0:65, c], resb_sb[0:65, :])]
                        else:
                            pe.wait_ge(gated, z_done.count(a, "yz"))
                            pairs = [(lambda c, j=j: y[:, j, c], wout_sb[:, j, :]) for j in range(DC)]
                            pairs += [(lambda c: tok(hT[b][0])[:, c], res0_sb[:]),
                                      (lambda c: tok(hT[b][1])[0:65, c], res1_sb[0:65, :])]
                        for t in (2 * k, 2 * k + 1):
                            for i, (lhs, rhs) in enumerate(pairs):
                                last = MM(PS[0:ROWS, bank(name), (t % 2) * EMB:(t % 2 + 1) * EMB], lhs(cols(t)), rhs,
                                          start=(i == 0), stop=(i == len(pairs) - 1))
                        last.then_inc(attn_pe, a_pe.step(name))
                if what == "h1T":
                    for m in range(2):
                        reader, count = last_read(a, f"h1T{m}")
                        if count is not None:
                            pe.wait_ge(reader, count)
                        for t in range(NTILE):
                            pe.wait_ge(attn_dve, a_dve.count(a, f"norm{t}"))
                            last = nc.tensor.transpose(PS[:, bank(f"h1T{m}"), cols(t)], h1[:, t, 128 * m:128 * m + 128],
                                                       id_sb[0:ROWS, 0:ROWS])
                        last.then_inc(attn_pe, a_pe.step(f"h1T{m}"))
                if what == "gate":
                    reader, count = last_read(a, "gate")
                    if count is not None:
                        pe.wait_ge(reader, count)
                    pe.wait_ge(attn_act, a_act.count(a, "h1T1"))
                    for t in range(NTILE):
                        dst = PS[0:ROWS, bank("gate"), NEXP * t:NEXP * t + NEXP]
                        MM(dst, h1T[0][:, cols(t)], wgate_sb[:, 0, :], start=True, stop=False)
                        last = MM(dst, h1T[1][0:65, cols(t)], wgate_sb[0:65, 1, :], start=False, stop=True)
                    last.then_inc(attn_pe, a_pe.step("gate"))
                    reader, count = last_read(a, "down")
                    if count is not None:
                        pe.wait_ge(reader, count)
                    MM(PS[:, bank("down"), 0:T], wdown_sb[:, 0, :], h1T[0][:], start=True, stop=False)
                    MM(PS[:, bank("down"), 0:T], wdown_sb[0:65, 1, :], h1T[1][0:65, :], start=False,
                                 stop=True).then_inc(attn_pe, a_pe.step("down"))
                if what == "spread":
                    reader, count = last_read(a, "spread")
                    if count is not None:
                        pe.wait_ge(reader, count)
                    pe.wait_ge(attn_dve, a_dve.count(a, "gwr"))
                    for t in range(NTILE):
                        last = MM(PS[:, bank("spread"), cols(t)], wrank[:, t * 128:(t + 1) * 128], id_sb[0:ROWS, 0:ROWS], start=True, stop=True)
                    last.then_inc(attn_pe, a_pe.step("spread"))
                if what == "v":
                    pe.wait_ge(attn_dve, a_dve.count(a, "aw"))
                    for k in range(2):
                        reader, count = last_read(a, f"v{k}")
                        if count is not None:
                            pe.wait_ge(reader, count)
                        for t in (2 * k, 2 * k + 1):
                            dst = PS[0:ROWS, bank(f"v{k}"), (t % 2) * EMB:(t % 2 + 1) * EMB]
                            MM(dst, h1T[0][:, cols(t)], wv_sb[:, 0, :], start=True, stop=False)
                            MM(dst, h1T[1][0:65, cols(t)], wv_sb[0:65, 1, :], start=False, stop=False)
                            last = MM(dst, aw[:, cols(t)], wv_sb[:, 2, :], start=False, stop=True)
                        last.then_inc(attn_pe, a_pe.step(f"v{k}"))
                if what[0] in "kq" and len(what) == 2:
                    m = int(what[1]) + (QC if what[0] == "k" else 0)
                    reader, count = last_read(a, what)
                    if count is not None:
                        pe.wait_ge(reader, count)
                    dst = PS[:, bank(what), 0:T]
                    w = slice(128 * m, 128 * m + 128)
                    MM(dst, wqk_sb[:, 0, w], h1T[0][:], start=True, stop=False)
                    MM(dst, wqk_sb[0:65, 1, w], h1T[1][0:65, :], start=False, stop=False)
                    MM(dst, wqk_sb[:, 2, w], aw[:], start=False, stop=True).then_inc(attn_pe, a_pe.step(what))
                if what[0] == "s" and what[1:].isdigit():
                    k = int(what[1:])
                    g, qt, hp = smax[k]
                    j = 2 * hp // QPC
                    reader, count = last_read(a, what)
                    if count is not None:
                        pe.wait_ge(reader, count)
                    pe.wait_ge(attn_act, a_act.count(a, f"q{j}"))
                    for i in range(2):
                        h = 2 * hp + i
                        last = MM(PS[0:ROWS, bank(what), i * LTOK:(i + 1) * LTOK], q[:, j, cols(2 * g + qt)],
                                  km[:, h, g * LTOK:(g + 1) * LTOK], start=True, stop=True)
                    last.then_inc(attn_pe, a_pe.step(what))
                if what == "m":
                    for j in range(QC):
                        reader, count = last_read(a, f"m{j}")
                        if count is not None:
                            pe.wait_ge(reader, count)
                        pe.wait_ge(attn_dve, a_dve.count(a, f"max{len(smax) - 1}"))
                        for t in range(NTILE):
                            last = nc.tensor.transpose(PS[:, bank(f"m{j}"), cols(t)], mpad[:, t, 128 * j:128 * j + 128],
                                                       id_sb[0:ROWS, 0:ROWS])
                        last.then_inc(attn_pe, a_pe.step(f"m{j}"))
                if what[0] == "t":
                    k, kt, hp = (int(c) for c in what[1:])
                    g, j = groups[k]
                    reader, count = last_read(a, what)
                    if count is not None:
                        pe.wait_ge(reader, count)
                    pe.wait_ge(attn_dve, a_dve.count(a, f"qm{QC - 1}"))
                    for i in range(2):
                        h = j * HPC + 2 * hp + i
                        last = MM(PS[0:ROWS, bank(what), i * LTOK:(i + 1) * LTOK], km[:, h, cols(2 * g + kt)],
                                  q[:, h // QPC, g * LTOK:(g + 1) * LTOK], start=True, stop=True)
                    last.then_inc(attn_pe, a_pe.step(what))
                if what[:2] == "pv":
                    k = int(what[2])
                    g, j = groups[k]
                    reader, count = last_read(a, what)
                    if count is not None:
                        pe.wait_ge(reader, count)
                    pe.wait_ge(attn_act, a_act.count(a, f"e{k}11"))
                    for kt in range(2):
                        for i in range(HPC):
                            last = MM(PS[HSLOT * i:HSLOT * (i + 1), bank(what), 0:LTOK],
                                      va[:, 2 * g + kt, j * HPC + i, :], pT[k % 2][:, kt, i, :],
                                      start=(kt == 0), stop=(kt == 1))
                    last.then_inc(attn_pe, a_pe.step(what))
                if what == "r":
                    for j in range(HC):
                        reader, count = last_read(a, f"r{j}")
                        if count is not None:
                            pe.wait_ge(reader, count)
                        pe.wait_ge(attn_act, a_act.count(a, f"o{len(groups) - 1}"))
                        MM(PS[:, bank(f"r{j}"), 0:T], swap_sb[:], o[:, j, :], start=True, stop=True).then_inc(attn_pe, a_pe.step(f"r{j}"))

            def part(f, s, a, z):
                if s:
                    b_row(s, 0)
                    b_row(s, 1)
                for n in steps:
                    if s:
                        if n + 2 < NST:
                            b_row(s, n + 2)
                        c_row(s, n)
                    for w, p in works(pe_plan, n, f, a, z):
                        (front if p is f else attn)(p, w)

            program(pe, None, part)


_NAMES = ["x", "w_patch", "pos", "cls", "b_patch", "w_in", "w_conv", "w_proj_bc", "w_proj_dt", "w_dt", "b_dt",
          "a_log", "d_param", "w_out", "w_qk", "w_v", "w_gate", "w_down", "w_o", "res0", "res1", "resb",
          "ident", "swap", "sel", "kmask", "vmask", "rev"]


def lay_out(np, i):
    f = {k: np.ascontiguousarray(v) for k, v in i.items()}

    def chunks(w, bias=None):
        k, n = w.shape
        kc = -(-k // 128)
        a = np.zeros((kc * 128, n), np.float32)
        a[:k] = w
        if bias is not None:
            a[k] = bias
        return np.ascontiguousarray(a.reshape(kc, 128, n).transpose(1, 0, 2))

    d = {}
    v = f["x"].reshape(NPAIR, G, SIDE, PATCH, SIDE, PATCH, CH)
    v = v.transpose(0, 6, 3, 5, 1, 2, 4).reshape(NPAIR, KP, 128, TP)
    d["x"] = np.ascontiguousarray(v.transpose(0, 2, 1, 3))
    d["w_patch"] = chunks(f["L0_tok_W"].T)
    d["pos"] = np.ascontiguousarray(f["L0_tok_pos_embed"][0].T)
    d["cls"] = chunks(f["L0_tok_cls_token"].reshape(EMB, 1))[:, :, 0]
    d["b_patch"] = chunks(f["L0_tok_b"].reshape(EMB, 1))[:, :, 0]
    d["w_in"] = chunks(f["L0_attn_w_in"].T)
    d["w_conv"] = chunks(f["L0_attn_w_conv"].reshape(DIN, NTAP))
    xp = f["L0_attn_w_xproj"]
    d["w_proj_bc"] = chunks(np.concatenate([xp[1:].T] * 3, axis=1))
    d["w_proj_dt"] = chunks(xp[0:1].T)
    d["w_dt"] = chunks(f["L0_attn_w_dt"])[:, :, 0]
    d["b_dt"] = chunks(f["L0_attn_b_dt"].reshape(DIN, 1))[:, :, 0]
    d["a_log"] = chunks(f["L0_attn_a_log"])
    d["d_param"] = chunks(f["L0_attn_d_param"].reshape(DIN, 1))[:, :, 0]
    d["w_out"] = chunks(f["L0_attn_w_out"].T)
    wq, bq = f["L0_ffn_W_qkv"].T, f["L0_ffn_b_qkv"]
    lora = f["L0_ffn_B_lora"].transpose(0, 2, 1).reshape(NEXP * RANK, 3 * EMB)

    def slots(w):
        a = np.zeros((w.shape[0], 2 * QC, 128), np.float32)
        a[:, :, :MROW] = w[:, :2 * EMB].reshape(w.shape[0], 2 * QC, MROW)
        return a

    bqk = slots(bq[None])
    bqk[:, QC:, MROW:MROW + QPC] = -1.0
    d["w_qk"] = np.concatenate([chunks(slots(wq).reshape(EMB, -1), bqk.reshape(-1)),
                                chunks(slots(lora).reshape(NEXP * RANK, -1))], axis=1)
    d["w_v"] = np.concatenate([chunks(wq[:, 2 * EMB:], bq[2 * EMB:]), chunks(lora[:, 2 * EMB:])], axis=1)
    d["w_gate"] = chunks(f["L0_ffn_W_gate"].T, f["L0_ffn_b_gate"])
    d["w_down"] = chunks(f["L0_ffn_A"].reshape(NEXP * RANK, EMB).T)
    wo = np.zeros((HEADS, HSLOT, EMB), np.float32)
    wo[:, :HD] = f["L0_ffn_W_proj"].T.reshape(HEADS, HD, EMB)
    d["w_o"] = chunks(wo.reshape(HEADS * HSLOT, EMB))
    eye = np.eye(EMB, dtype=np.float32)
    d["res0"] = eye[:128]
    d["res1"] = np.concatenate([eye[128:], np.zeros((64, EMB), np.float32)])
    d["resb"] = np.concatenate([eye[128:], f["L0_ffn_b_proj"][None], np.zeros((63, EMB), np.float32)])
    d["ident"] = np.eye(128, dtype=np.float32)
    s = np.zeros((128, 128), np.float32)
    for m in range(128):
        s[m // HSLOT * HSLOT + HD + m % HD, m] = 1.0
    d["swap"] = s
    s = np.zeros((96, 2 * NST, 128), np.float32)
    for r in range(96):
        s[r, r % 32] = 1.0
    d["sel"] = s.reshape(96, -1)
    km = np.zeros((128, QPC), np.float32)
    for i in range(QPC):
        km[HD * i:HD * i + HD, i] = km[MROW + i, i] = 1.0
    d["kmask"] = km
    vm = np.ones((ROWS, 1), np.float32)
    vm[0] = 0.0
    d["vmask"] = vm
    d["rev"] = np.broadcast_to(np.arange(NEXP, 0, -1, dtype=np.float32), (ROWS, NTILE, NEXP))
    return {k: np.ascontiguousarray(d[k]) for k in _NAMES}


def kernel(**inputs):
    import numpy as _np
    import concourse.bacc as _bacc
    from concourse import mybir as _mybir
    from concourse.bass_utils import run_bass_kernel_spmd as _run

    nc = _bacc.Bacc("TRN2", target_bir_lowering=False, num_devices=1)
    laid = lay_out(_np, {k: _np.asarray(v) for k, v in inputs.items()})
    arrays, args = {}, []
    for name, a in laid.items():
        arrays[f"in_{name}_dram"] = a
        args.append(nc.dram_tensor(f"in_{name}_dram", a.shape, _mybir.dt.from_np(a.dtype), kind="ExternalInput").ap())
    args.append(nc.dram_tensor("out_0_dram", (NPAIR, G, LTOK, EMB), _mybir.dt.float32, kind="ExternalOutput").ap())
    tower_kernel(nc, *args)
    r = _run(nc, [arrays], core_ids=[0])
    return r.results[0]["out_0_dram"].reshape(NB, LTOK, EMB)
```

```python
import concourse.bass as bass
from concourse import mybir
from contextlib import ExitStack

NB, SIDE, PATCH, CH = 64, 14, 16, 3
EMB, DIN, NST, NTAP = 192, 384, 16, 4
NEXP, RANK, ALPHA = 8, 16, 32
HEADS, HD = 12, 16
LTOK = SIDE * SIDE + 1
NPATCH = SIDE * SIDE
G = 2
NPAIR = NB // G
T = G * LTOK
TP = G * NPATCH
KP = CH * PATCH * PATCH // 128
DC = DIN // 128
ROWS = (LTOK + 1) // 2
NTILE = 2 * G
HSLOT = 32
HPC = 128 // HSLOT
HC = HEADS // HPC
QPC = 6
QC = HEADS // QPC
MROW = QPC * HD
PADW = 256
SCALE = float(HD) ** -0.5
EPS = 1e-5
LN_EXP_TABLES, SILU_TABLES = 6, 18


class Pair:

    def __init__(self, j, off):
        self.j, self.off = j, off

    def plus(self, d):
        return Pair(self.j, self.off + d)

    @property
    def parity(self):
        return self.off % 2

    def has(self, d):
        return self.j is not None or self.off + d >= 0

    @property
    def exists(self):
        return self.j is not None or 0 <= self.off < NPAIR

    def times(self, k, c):
        v = self.off * k + c
        return v if self.j is None else self.j * (2 * k) + v


class Order:

    def __init__(self, names):
        self.names = list(names)
        self.at = {n: k for k, n in enumerate(self.names)}
        assert len(self.at) == len(self.names)
        self.n = 0

    def step(self, name):
        assert self.names[self.n % len(self.names)] == name, (name, self.names[self.n % len(self.names)])
        self.n += 1
        return 1

    def count(self, pair, name):
        return pair.times(len(self.names), self.at[name] + 1)


def tower_kernel(nc, x, w_patch, pos, cls, b_patch, w_in, w_conv, w_proj_bc, w_proj_dt, w_dt, b_dt,
                 a_log, d_param, w_out, w_qk, w_v, w_gate, w_down, w_o, res0, res1,
                 ident, swap, sel, kmask, vmask, rev, out):
    fp32, bf16 = mybir.dt.float32, mybir.dt.bfloat16
    ALU = mybir.AluOpType
    ACT = mybir.ActivationFunctionType
    AX = mybir.AxisListType

    ctx = ExitStack()
    with ctx:
        def sb(name, shape, dt=fp32):
            return ctx.enter_context(nc.sbuf_tensor(name, shape, dt))

        def sem(name):
            return ctx.enter_context(nc.semaphore(name))

        wpatch_sb = sb("wpatch_sb", [128, KP, EMB])
        pos_sb = sb("pos_sb", [128, 2, LTOK])
        cls_sb = sb("cls_sb", [128, 2])
        bp_sb = sb("bp_sb", [128, 2])
        win_sb = sb("win_sb", [128, 2, 2 * DIN])
        conv_sb = sb("conv_sb", [128, DC, NTAP])
        wbc_sb = sb("wbc_sb", [128, DC, 96])
        wraw_sb = sb("wraw_sb", [128, DC, 1])
        wdt_sb = sb("wdt_sb", [128, DC])
        bdt_sb = sb("bdt_sb", [128, DC])
        negA = sb("negA", [128, DC, NST])
        d_sb = sb("d_sb", [128, DC])
        wout_sb = sb("wout_sb", [128, DC, EMB])
        wqk_sb = sb("wqk_sb", [128, 3, 2 * QC * 128])
        wv_sb = sb("wv_sb", [128, 3, EMB])
        wgate_sb = sb("wgate_sb", [128, 2, NEXP])
        wdown_sb = sb("wdown_sb", [128, 2, 128])
        wo_sb = sb("wo_sb", [128, HC, EMB])
        res0_sb = sb("res0_sb", [128, EMB])
        res1_sb = sb("res1_sb", [128, EMB])
        id_sb = sb("id_sb", [128, 128])
        swap_sb = sb("swap_sb", [128, 128])
        sel_f32 = sb("sel_f32", [96, 2 * NST])
        sel_sb = sb("sel_sb", [96, 2 * NST], bf16)
        kmask_sb = sb("kmask_sb", [128, QPC])
        vmask_sb = sb("vmask_sb", [ROWS, 1])
        rev_sb = sb("rev_sb", [ROWS, NTILE, NEXP])

        xin = sb("xin", [128, KP, TP])
        hT = [[sb(f"hT{m}_{b}", [128, G, LTOK]) for m in range(2)] for b in range(2)]
        xpad = sb("xpad", [128, DC, G, LTOK + 3])
        cv = sb("cv", [128, DC, T])
        ex = sb("ex", [128, DC, T])
        xs = [sb(f"xs{b}", [128, DC, T]) for b in range(2)]
        sz = [sb(f"sz{b}", [128, DC, T]) for b in range(2)]
        dt = [sb(f"dt{b}", [128, DC, T]) for b in range(2)]
        dtx = [sb(f"dtx{b}", [128, DC, T]) for b in range(2)]
        bc = [sb(f"bc{b}", [96, T], bf16) for b in range(2)]
        bcrest = sb("bcrest", [64, T])
        NA, NU = 2, 4
        abar = [sb(f"abar{k}", [128, DC, G, LTOK]) for k in range(NA)]
        state = [sb(f"state{k}", [128, DC, T]) for k in range(NU)]
        b_sb = sb("b_sb", [128, 1, T])
        yacc = sb("yacc", [128, DC, T])
        y = sb("y", [128, DC, T])
        st = [sb(f"st{k}", [ROWS, NTILE, 6]) for k in range(2)]
        mv = [sb(f"mv{k}", [ROWS, NTILE, 2]) for k in range(2)]
        rs = [sb(f"rs{k}", [ROWS, NTILE]) for k in range(2)]
        shift = [sb(f"shift{k}", [ROWS, NTILE]) for k in range(2)]
        h1 = [sb(f"h1_{b}", [ROWS, NTILE, PADW]) for b in range(2)]
        h1T = [sb(f"h1T{m}", [128, T]) for m in range(2)]
        gk = [sb(f"gk{k}", [ROWS, NTILE, NEXP]) for k in range(5)]
        gs = sb("gs", [ROWS, NTILE])
        ad = sb("ad", [128, T])
        aw = sb("aw", [128, T])
        km = sb("km", [128, HEADS, T])
        q = sb("q", [128, QC, T])
        va = sb("va", [ROWS, NTILE, HEADS, HSLOT])
        mpad = sb("mpad", [ROWS, NTILE, QC * 128])
        pT = [sb(f"pT{k}", [ROWS, 2, HPC, LTOK]) for k in range(2)]
        wrank = pT[0][:].rearrange("p k h t -> p (k h t)")[:, 0:NTILE * 128]
        o = sb("o", [128, HC, T])
        rinv = km[:, 0:HC, :]
        fin = pT[1][:].rearrange("p k h t -> p (k h t)")[:, 0:NTILE * EMB].rearrange("p (t e) -> p t e", e=EMB)
        eps_sb = sb("eps_sb", [ROWS, 1])
        square_sb = sb("square_sb", [128, 1])

        PS = ctx.enter_context(nc.psum_tensor("PS", [128, 8, 512], fp32))
        BB, CB, AB, FB = 0, 2, 4, 7
        NBC, NAB = 2, 3

        s_first = sem("s_first")
        s_load = sem("s_load")
        s_cast = sem("s_cast")
        s_setup = sem("s_setup")
        s_x = sem("s_x")
        s_apart = sem("s_apart")
        s_out = sem("s_out")

        steps = range(NST)
        LEAD = 1
        POOL_TERMS = (3, 5, 7, 9)
        front_pe = sem("front_pe")
        f_pe = Order(["patch0", "patch1"] + [f"xz{m}" for m in range(6)] + ["raw", "bc"])
        front_act = sem("front_act")
        f_act = Order([f"xz{m}" for m in range(6)] + ["xs", "sz"]
                      + [f"abs{c}" for c in range(DC)] + [f"relu{c}" for c in range(DC)] + ["ep", "square", "lp"])
        SMALL = 2.0 ** -6
        front_dve = sem("front_dve")
        f_dve = Order(["hT0", "hT1"] + [f"conv{c}{j}" for c in range(DC) for j in range(NTAP)]
                      + [f"split{k}" for k in range(5)] + ["chosen"])
        front_pool = sem("front_pool")
        f_pool = Order(["series", "small", "large", "dt", "dtx"])
        b_broadcast = sem("b_broadcast")
        b_done = Order(steps)
        c_broadcast = sem("c_broadcast")
        c_done = Order(steps)
        state_summed = sem("state_summed")
        n_done = Order(steps)
        skip_term = sem("skip_term")
        k_done = Order(range(DC))
        input_term = sem("input_term")
        u_done = Order([n for n in steps if n not in POOL_TERMS])
        b_copied = sem("b_copied")
        bc_done = Order(POOL_TERMS)
        pool_term = sem("pool_term")
        pu_done = Order(POOL_TERMS)
        scanned = sem("scanned")
        h_done = Order(steps)
        c_applied = sem("c_applied")
        hc_done = Order(steps)
        decayed = sem("decayed")
        a_done = Order(steps)

        groups = [(g, j) for g in range(G) for j in range(HC)]
        smax = [(g, qt, hp) for g in range(G) for qt in range(2) for hp in range(HEADS // 2)]
        uses = [("out0", "a", "norm1"), ("out1", "a", "norm3"), ("proj0", "z", "res0"), ("proj1", "z", "res1"),
                ("h1T0", "a", "h1T0"), ("h1T1", "a", "h1T1"),
                ("gate", "d", "gd"), ("down", "a", "down"), ("spread", "d", "aw"),
                ("v0", "a", "v1"), ("v1", "a", "v3")]
        for j in range(QC):
            uses += [(f"k{j}", "a", f"k{j}{QPC - 1}"), (f"q{j}", "a", f"q{j}")]
        uses += [(f"s{k}", "d", f"max{k}") for k in range(len(smax))]
        uses += [(f"m{j}", "d", f"qm{j}") for j in range(QC)]
        seq = []
        for k in range(len(groups) + 1):
            if k < len(groups):
                seq += [("t", k, kt, hp) for kt in range(2) for hp in range(2)]
            if k >= 1:
                seq += [("pv", k - 1)]
        for s in seq:
            uses.append(("t%d%d%d" % s[1:], "a", "e%d%d%d" % s[1:]) if s[0] == "t" else (f"pv{s[1]}", "a", f"o{s[1]}"))
        uses += [(f"r{j}", "a", f"lr{j}") for j in range(HC)]
        turn = {u[0]: k for k, u in enumerate(uses)}

        gated = sem("gated")
        z_done = Order(["yz"])
        attn_pe = sem("attn_pe")
        a_pe = Order([u[0] for u in uses if u[1] != "z"])
        end_pe = sem("end_pe")
        z_pe = Order(["proj0", "proj1"])
        end_act = sem("end_act")
        z_act = Order(["ln2", "ln3"] + [f"fin{t}" for t in range(NTILE)])
        end_pool = sem("end_pool")
        z_pool = Order(["on"])
        end_dve = sem("end_dve")
        z_dve = Order(["res0", "res1"] + [f"ft{t}" for t in range(NTILE)] + [f"fv{t}" for t in range(NTILE)] + ["shift"])
        attn_act = sem("attn_act")
        a_act = Order(["ln0", "ln1"] + [f"norm{t}" for t in range(NTILE)] + ["h1T0", "h1T1", "ge", "down"]
                      + [f"v{t}" for t in range(NTILE)]
                      + [n for j in range(QC) for n in [f"k{j}{i}" for i in range(QPC)] + [f"q{j}"]]
                      + [("e%d%d%d" % s[1:]) if s[0] == "t" else f"o{s[1]}" for s in seq]
                      + [f"lr{j}" for j in range(HC)] + ["er"])
        attn_dve = sem("attn_dve")
        a_dve = Order([f"st{t}" for t in range(NTILE)] + [f"mv{t}" for t in range(NTILE)]
                      + ["shift", "gmx", "gd", "gs", "gr", "gp"]
                      + [f"{a}0" for a in ("gm", "ge", "gc", "gt", "go")] + ["gx"]
                      + [f"{a}1" for a in ("gm", "ge", "gc", "gt", "go")] + ["gu", "gw", "gwr", "aw"]
                      + [f"max{k}" for k in range(len(smax))] + [f"qm{j}" for j in range(QC)])

        def apart(engine):
            engine.sem_inc(s_apart, 1)

        def bank(name):
            return AB + turn[name] % NAB

        def last_read(p, name):
            for d in (0, -1, -2):
                for i in reversed(range(turn[name] if d == 0 else len(uses))):
                    _, who, what = uses[i]
                    owner = p.plus(d - 1 if who == "z" else d)
                    if i % NAB != turn[name] % NAB or not owner.exists:
                        continue
                    if who == "z":
                        return end_dve, z_dve.count(owner, what)
                    if who == "a":
                        return attn_act, a_act.count(owner, what)
                    return attn_dve, a_dve.count(owner, what)
            return attn_dve, None

        def term_read(p, n):
            if n in POOL_TERMS:
                return pool_term, pu_done.count(p, n)
            return input_term, u_done.count(p, n)

        def b_read(p, n):
            if n in POOL_TERMS:
                return b_copied, bc_done.count(p, n)
            return input_term, u_done.count(p, n)

        def cols(tile):
            g, qt = tile // 2, tile % 2
            a = g * LTOK + qt * (LTOK - ROWS)
            return slice(a, a + ROWS)

        def flat(t):
            return t[:, :, :].rearrange("p c t -> p (c t)")

        def tok(h):
            return h[:, :, :].rearrange("p g t -> p (g t)")

        score_plan = [f"s{k}" for k in range(len(smax))]
        value_plan = [("t%d%d%d" % s[1:]) if s[0] == "t" else f"pv{s[1]}" for s in seq]

        FRONT = {"patch", "xz", "conv", "silu", "raw", "series", "bc", "log", "large", "chosen"}
        TAIL = {"on", "proj", "res", "fin"}
        pe_plan = {0: ["patch0", "out0", "out1"], 1: ["proj", "patch1"], 2: ["h1T"],
                   3: ["gate", "xz0", "spread"], 4: ["v", "k0", "q0", "xz1"], 5: ["k1", "q1", "xz2", "xz3"],
                   6: score_plan[0:3] + ["xz4"] + score_plan[3:6] + ["xz5"], 7: score_plan[6:10],
                   8: ["raw"] + score_plan[10:14], 9: score_plan[14:18] + ["bc"] + score_plan[18:24],
                   10: ["m"] + value_plan[0:8], 11: value_plan[8:14], 12: value_plan[14:20],
                   13: value_plan[20:26], 14: value_plan[26:28], 15: value_plan[28:30] + ["r"]}
        act_plan = {1: ["norm"], 2: ["h1T"], 3: ["gate"], 4: ["v", "xz0", "fin", "k0", "q0", "xz1"],
                    5: ["k1", "q1", "xz2", "xz3"], 6: ["xz4", "xz5"], 7: ["silu"], 8: ["raw"], 9: ["t000"],
                    10: ["log"] + value_plan[1:8], 11: value_plan[8:17], 12: value_plan[17:23],
                    13: value_plan[23:26], 14: value_plan[26:30], 15: ["r"]}
        dve_plan = {0.6: ["yz"], 1.6: ["norm", "patch0"], 2: ["res"], 2.6: ["patch1"], 3: ["gate"],
                    3.3: ["aw"], 4: ["fin"], 4.6: ["conv0"], 5.6: ["conv1", "conv2"], 6.3: score_plan[0:3],
                    6.6: score_plan[3:6], 7: score_plan[6:9], 7.3: ["s9"], 8.3: score_plan[10:12],
                    8.6: score_plan[12:15], 9: score_plan[15:18], 9.3: score_plan[18:22],
                    9.6: score_plan[22:24] + ["m"], 10.3: ["bc"], 11.6: ["chosen"]}
        pool_plan = {0: ["on"], 9: ["series"], 10: ["large"], 12: ["chosen"]}

        def works(plan, n, f, a, z):
            for w in plan.get(n, []):
                p = z if w in TAIL else f if w.rstrip("0123456789") in FRONT else a
                if p:
                    yield w, p

        def program(engine, loop, part):
            def it(j, i, f=True, s=True, a=True, z=True):
                part(Pair(j, i + 1) if f else None, Pair(j, i) if s else None,
                     Pair(j, i - 1) if a else None, Pair(j, i - 2) if z else None)

            it(None, -1, s=False, a=False, z=False)
            it(None, 0, a=False, z=False)
            it(None, 1, z=False)
            it(None, 2)
            with engine.Fori(1, (NPAIR - 2) // 2) as j:
                it(j, 1)
                it(j, 2)
            it(None, NPAIR - 1, f=False)
            it(None, NPAIR, f=False, s=False)
            it(None, NPAIR + 1, f=False, s=False, a=False)

        NFIRST, NLOADS = 5, 21
        block = ctx.enter_context(nc.Block())

        @block.sync
        def _(sp):
            loads = [(pos_sb[:], pos), (cls_sb[:], cls),
                     (bp_sb[:], b_patch), (wpatch_sb[:], w_patch), (win_sb[:], w_in)]
            assert len(loads) == NFIRST
            for dst, src in loads:
                sp.dma_start(dst, src).then_inc(s_first, 16)

            def part(f, s, a, z):
                if f:
                    if f.has(-1):
                        sp.wait_ge(front_pe, f_pe.count(f.plus(-1), "patch1"))
                    src = x[f.off] if f.j is None else x[f.j * 2 + f.off]
                    sp.dma_start(xin[:], src).then_inc(s_x, 16)
                if z:
                    sp.wait_ge(end_act, z_act.count(z, "fin3"))
                    dst = out[z.off] if z.j is None else out[z.j * 2 + z.off]
                    sp.dma_start(dst[:, 0:ROWS, :].rearrange("g t e -> t g e"),
                                 fin[:, 0:NTILE:2, :]).then_inc(s_out, 16)
                    sp.dma_start(dst[:, ROWS:LTOK, :].rearrange("g t e -> t g e"),
                                 fin[1:ROWS, 1:NTILE:2, :]).then_inc(s_out, 16)

            program(sp, None, part)
            sp.wait_ge(s_out, 32 * NPAIR)

        @block.gpsimd
        def _(pool):
            pool.wait_ge(s_setup, 4)

            def add_state(p, n):
                if n == 0:
                    pool.wait_ge(skip_term, k_done.count(p, DC - 1))
                else:
                    pool.wait_ge(state_summed, n_done.count(p, n - 1))
                pool.wait_ge(c_applied, hc_done.count(p, n))
                nc.gpsimd.tensor_tensor(flat(yacc), flat(yacc), flat(state[n % NU]),
                                        ALU.add).then_inc(state_summed, n_done.step(n))

            def term(p, n):
                pool.wait_ge(b_copied, bc_done.count(p, n))
                if n >= NU:
                    pool.wait_ge(state_summed, n_done.count(p, n - NU))
                elif p.has(-1):
                    pool.wait_ge(state_summed, n_done.count(p.plus(-1), NST + n - NU))
                nc.gpsimd.tensor_tensor(state[n % NU][:], dtx[p.parity][:], b_sb[:].to_broadcast([128, DC, T]),
                                        ALU.mult).then_inc(pool_term, pu_done.step(n))

            def end(z, what):
                pool.wait_ge(attn_act, a_act.count(z, "er"))
                nc.gpsimd.tensor_tensor(flat(o), flat(o), flat(rinv), ALU.mult).then_inc(end_pool, z_pool.step("on"))

            def front(f, what):
                b = f.parity
                if what == "large":
                    pool.wait_ge(front_act, f_act.count(f, "lp"))
                    apart(pool)
                    nc.gpsimd.tensor_scalar(flat(ex), flat(ex), -SMALL, 0.0, ALU.add,
                                            ALU.max).then_inc(front_pool, f_pool.step("large"))
                if what == "series":
                    pool.wait_ge(front_act, f_act.count(f, "square"))
                    apart(pool)
                    nc.gpsimd.tensor_scalar(flat(dtx[b]), flat(dtx[b]), 1.0 / 3, 1.0 - 9.0 / 48, ALU.mult,
                                            ALU.add).then_inc(front_pool, f_pool.step("series"))
                    pool.wait_ge(front_pool, f_pool.count(f, "series"))
                    if f.has(-2):
                        pool.wait_ge(decayed, a_done.count(f.plus(-2), NST - 1))
                    nc.gpsimd.tensor_tensor(flat(dt[b]), flat(dtx[b]), flat(ex),
                                            ALU.mult).then_inc(front_pool, f_pool.step("small"))
                if what == "chosen":
                    pool.wait_ge(front_dve, f_dve.count(f, "chosen"))
                    nc.gpsimd.tensor_tensor(flat(dt[b]), flat(dt[b]), flat(cv),
                                            ALU.add).then_inc(front_pool, f_pool.step("dt"))
                    pool.wait_ge(front_pool, f_pool.count(f, "dt"))
                    nc.gpsimd.tensor_tensor(flat(dtx[b]), flat(dt[b]), flat(xs[b]),
                                            ALU.mult).then_inc(front_pool, f_pool.step("dtx"))

            def part(f, s, a, z):
                for n in steps:
                    if s and n + 1 in POOL_TERMS:
                        term(s, n + 1)
                    if s and n >= 1:
                        add_state(s, n - 1)
                    for w, p in works(pool_plan, n, f, a, z):
                        (front if p is f else end)(p, w)
                if s:
                    add_state(s, NST - 1)

            program(pool, None, part)

        @block.scalar
        def _(act):
            loads = [(conv_sb[:], w_conv), (negA[:], a_log), (sel_f32[:], sel),
                     (wbc_sb[:], w_proj_bc), (wraw_sb[:], w_proj_dt), (wdt_sb[:], w_dt), (bdt_sb[:], b_dt),
                     (d_sb[:], d_param), (wout_sb[:], w_out), (wqk_sb[:], w_qk),
                     (wv_sb[:], w_v), (wgate_sb[:], w_gate), (wdown_sb[:], w_down), (wo_sb[:], w_o),
                     (res0_sb[:], res0), (res1_sb[:], res1), (id_sb[:], ident),
                     (swap_sb[:], swap), (kmask_sb[:], kmask), (vmask_sb[:], vmask), (rev_sb[:], rev)]
            assert len(loads) == NLOADS
            for dst, src in loads:
                act.dma_start(dst, src).then_inc(s_load, 16)
            act.wait_ge(s_load, 16 * NLOADS)

            def tables(number):
                nc.scalar.add_instruction(mybir.InstLoadActFuncSet(
                    name=nc.get_next_instruction_name(), engine=mybir.EngineType.Activation,
                    act_func_set_id=number, ins=[], outs=[]))

            tables(LN_EXP_TABLES)
            nc.scalar.activation(negA[:], negA[:], ACT.Exp).then_inc(s_cast, 1)

            def decay(p, n):
                if n == 0:
                    act.wait_ge(front_pool, f_pool.count(p, "dt"))
                if n >= NA:
                    act.wait_ge(scanned, h_done.count(p, n - NA))
                else:
                    if p.has(-1):
                        act.wait_ge(scanned, h_done.count(p.plus(-1), NST + n - NA))
                b = p.parity
                for c in range(DC):
                    last = nc.scalar.activation(
                        abar[n % NA][:, c, :, 1:], dt[b][:, c, :].rearrange("p (g t) -> p g t", g=G)[:, :, 1:],
                        ACT.Exp, scale=negA[:, c, n:n + 1])
                last.then_inc(decayed, a_done.step(n))

            def copy_b(p, n):
                act.wait_ge(b_broadcast, b_done.count(p, n))
                k = POOL_TERMS.index(n)
                if k:
                    act.wait_ge(pool_term, pu_done.count(p, POOL_TERMS[k - 1]))
                elif p.has(-1):
                    act.wait_ge(pool_term, pu_done.count(p.plus(-1), POOL_TERMS[-1]))
                nc.scalar.activation(b_sb[:, 0, :], PS[:, BB + n % NBC, 0:T],
                                     ACT.Copy).then_inc(b_copied, bc_done.step(n))

            def skip(p):
                if p.has(-1):
                    act.wait_ge(gated, z_done.count(p.plus(-1), "yz"))
                for c in range(DC):
                    nc.scalar.activation(yacc[:, c, :], xs[p.parity][:, c, :], ACT.Copy,
                                         scale=d_sb[:, c:c + 1]).then_inc(skip_term, k_done.step(c))

            def front(f, what):
                fbank = PS[:, FB, 0:T]
                if what[:2] == "xz":
                    m = int(what[2])
                    act.wait_ge(front_pe, f_pe.count(f, what))
                    if m < DC:
                        if f.has(-1):
                            act.wait_ge(front_dve, f_dve.count(f.plus(-1), f"conv{DC - 1}{NTAP - 1}"))
                        nc.scalar.activation(xpad[:, m, :, 3:], fbank.rearrange("p (g t) -> p g t", g=G),
                                                        ACT.Copy).then_inc(front_act, f_act.step(what))
                    else:
                        if f.has(-2):
                            act.wait_ge(gated, z_done.count(f.plus(-2), "yz"))
                        nc.scalar.activation(sz[f.parity][:, m - DC, :], fbank, ACT.Copy).then_inc(front_act, f_act.step(what))
                if what == "silu":
                    b = f.parity
                    tables(SILU_TABLES)
                    act.wait_ge(front_dve, f_dve.count(f, f"conv{DC - 1}{NTAP - 1}"))
                    if f.has(-2):
                        act.wait_ge(skip_term, k_done.count(f.plus(-2), DC - 1))
                    act.wait_ge(front_act, f_act.count(f, "xz5"))
                    nc.scalar.activation(flat(xs[b]), flat(cv), ACT.Silu).then_inc(front_act, f_act.step("xs"))
                    nc.scalar.activation(flat(sz[b]), flat(sz[b]), ACT.Silu).then_inc(front_act, f_act.step("sz"))
                    tables(LN_EXP_TABLES)
                if what == "raw":
                    act.wait_ge(front_pe, f_pe.count(f, "raw"))
                    act.wait_ge(front_act, f_act.count(f, "xs"))
                    if f.has(-1):
                        act.wait_ge(front_pool, f_pool.count(f.plus(-1), "dtx"))
                    for c in range(DC):
                        nc.scalar.activation(ex[:, c, :], fbank, ACT.Abs, scale=wdt_sb[:, c:c + 1],
                                                        bias=bdt_sb[:, c:c + 1]).then_inc(front_act, f_act.step(f"abs{c}"))
                    for c in range(DC):
                        nc.scalar.activation(cv[:, c, :], fbank, ACT.Relu, scale=wdt_sb[:, c:c + 1],
                                                        bias=bdt_sb[:, c:c + 1]).then_inc(front_act, f_act.step(f"relu{c}"))
                    act.wait_ge(front_act, f_act.count(f, f"abs{DC - 1}"))
                    nc.scalar.activation(flat(ex), flat(ex), ACT.Exp, scale=-1.0).then_inc(front_act, f_act.step("ep"))
                    act.wait_ge(front_act, f_act.count(f, "ep"))
                    if f.has(-2):
                        act.wait_ge(pool_term, pu_done.count(f.plus(-2), POOL_TERMS[-1]))
                        act.wait_ge(input_term, u_done.count(f.plus(-2), NST - 1))
                    nc.scalar.activation(flat(dtx[f.parity]), flat(ex), ACT.Square,
                                         bias=square_sb[:]).then_inc(front_act, f_act.step("square"))
                if what == "log":
                    act.wait_ge(front_pool, f_pool.count(f, "small"))
                    nc.scalar.activation(flat(dtx[f.parity]), flat(ex), ACT.Ln, bias=1.0).then_inc(front_act, f_act.step("lp"))

            def attn(a, what):
                if what == "norm":
                    act.wait_ge(attn_dve, a_dve.count(a, f"mv{NTILE - 1}"))
                    nc.scalar.activation(rs[0][:], mv[0][:, :, 1], ACT.Ln, bias=eps_sb[:]).then_inc(attn_act, a_act.step("ln0"))
                    act.wait_ge(attn_act, a_act.count(a, "ln0"))
                    nc.scalar.activation(rs[0][:], rs[0][:], ACT.Exp, scale=-0.5).then_inc(attn_act, a_act.step("ln1"))
                    if a.has(-2):
                        act.wait_ge(end_dve, z_dve.count(a.plus(-2), "res1"))
                    act.wait_ge(attn_dve, a_dve.count(a, "shift"))
                    for t in range(NTILE):
                        nc.scalar.activation(
                            h1[a.parity][:, t, 0:EMB], PS[0:ROWS, bank(f"out{t // 2}"), (t % 2) * EMB:(t % 2 + 1) * EMB],
                            ACT.Identity, scale=rs[0][:, t:t + 1],
                            bias=shift[0][:, t:t + 1]).then_inc(attn_act, a_act.step(f"norm{t}"))
                if what == "fin":
                    act.wait_ge(end_dve, z_dve.count(a, f"fv{NTILE - 1}"))
                    nc.scalar.activation(rs[1][:], mv[1][:, :, 1], ACT.Ln, bias=eps_sb[:]).then_inc(end_act, z_act.step("ln2"))
                    act.wait_ge(end_act, z_act.count(a, "ln2"))
                    nc.scalar.activation(rs[1][:], rs[1][:], ACT.Exp, scale=-0.5).then_inc(end_act, z_act.step("ln3"))
                    act.wait_ge(end_dve, z_dve.count(a, "shift"))
                    for t in range(NTILE):
                        nc.scalar.activation(
                            fin[:, t, :], fin[:, t, :], ACT.Identity, scale=rs[1][:, t:t + 1],
                            bias=shift[1][:, t:t + 1]).then_inc(end_act, z_act.step(f"fin{t}"))
                if what == "h1T":
                    for m in range(2):
                        act.wait_ge(attn_pe, a_pe.count(a, f"h1T{m}"))
                        if m == 0 and a.has(-1):
                            act.wait_ge(attn_pe, a_pe.count(a.plus(-1), f"q{QC - 1}"))
                        nc.scalar.activation(h1T[m][:], PS[:, bank(f"h1T{m}"), 0:T], ACT.Copy).then_inc(attn_act, a_act.step(f"h1T{m}"))
                if what == "gate":
                    act.wait_ge(attn_dve, a_dve.count(a, "gd"))
                    nc.scalar.activation(gk[0][:], gk[0][:], ACT.Exp).then_inc(attn_act, a_act.step("ge"))
                    act.wait_ge(attn_pe, a_pe.count(a, "down"))
                    nc.scalar.activation(ad[:], PS[:, bank("down"), 0:T], ACT.Copy).then_inc(attn_act, a_act.step("down"))
                if what == "v":
                    for t in range(NTILE):
                        if t % 2 == 0:
                            act.wait_ge(attn_pe, a_pe.count(a, f"v{t // 2}"))
                        src = PS[0:ROWS, bank(f"v{t // 2}"), (t % 2) * EMB:(t % 2 + 1) * EMB]
                        nc.scalar.activation(va[:, t, :, 0:HD], src.rearrange("p (h d) -> p h d", d=HD),
                                                        ACT.Copy, scale=vmask_sb[:] if t % 2 else 1.0).then_inc(attn_act, a_act.step(f"v{t}"))
                if what[0] == "k" and len(what) == 2:
                    j = int(what[1])
                    act.wait_ge(attn_pe, a_pe.count(a, what))
                    for i in range(QPC):
                        nc.scalar.activation(km[:, j * QPC + i, :], PS[:, bank(what), 0:T], ACT.Copy,
                                                        scale=kmask_sb[:, i:i + 1]).then_inc(attn_act, a_act.step(f"k{j}{i}"))
                if what[0] == "q" and len(what) == 2:
                    j = int(what[1])
                    act.wait_ge(attn_pe, a_pe.count(a, what))
                    nc.scalar.activation(q[:, j, :], PS[:, bank(what), 0:T], ACT.Copy).then_inc(attn_act, a_act.step(what))
                if what[0] == "t":
                    k, kt, hp = (int(c) for c in what[1:])
                    act.wait_ge(attn_pe, a_pe.count(a, what))
                    if what == "t100" and a.has(-1):
                        act.wait_ge(s_out, a.times(32, 0))
                    if k >= 2:
                        act.wait_ge(attn_pe, a_pe.count(a, f"pv{k - 2}"))
                    else:
                        if a.has(-1):
                            act.wait_ge(attn_pe, a_pe.count(a.plus(-1), f"pv{len(groups) + k - 2}"))
                    nc.scalar.activation(
                        pT[k % 2][:, kt, 2 * hp:2 * hp + 2, :].rearrange("p h t -> p (h t)"),
                        PS[0:ROWS, bank(what), 0:T], ACT.Exp, scale=SCALE).then_inc(attn_act, a_act.step("e" + what[1:]))
                if what[:2] == "pv":
                    k = int(what[2])
                    g, j = groups[k]
                    act.wait_ge(attn_pe, a_pe.count(a, what))
                    if k == 0:
                        if a.has(-1):
                            act.wait_ge(end_pe, z_pe.count(a.plus(-1), "proj1"))
                    nc.scalar.activation(o[:, j, g * LTOK:(g + 1) * LTOK], PS[:, bank(what), 0:LTOK],
                                                    ACT.Copy).then_inc(attn_act, a_act.step(f"o{k}"))
                if what == "r":
                    for j in range(HC):
                        act.wait_ge(attn_pe, a_pe.count(a, f"r{j}"))
                        nc.scalar.activation(rinv[:, j, :], PS[:, bank(f"r{j}"), 0:T], ACT.Ln).then_inc(attn_act, a_act.step(f"lr{j}"))
                    act.wait_ge(attn_act, a_act.count(a, f"lr{HC - 1}"))
                    nc.scalar.activation(flat(rinv), flat(rinv), ACT.Exp, scale=-1.0).then_inc(attn_act, a_act.step("er"))

            act.wait_ge(s_setup, 4)

            def part(f, s, a, z):
                for n in range(LEAD if s else 0):
                    decay(s, n)
                for n in steps:
                    if s and n + 1 in POOL_TERMS:
                        copy_b(s, n + 1)
                    if s and n + LEAD < NST:
                        decay(s, n + LEAD)
                    if s and n == 1:
                        skip(s)
                    for w, p in works(act_plan, n, f, a, z):
                        (front if p is f else attn)(p, w)

            program(act, None, part)

        @block.vector
        def _(dve):
            TT, TS, STT = nc.vector.tensor_tensor, nc.vector.tensor_scalar, nc.vector.scalar_tensor_tensor
            nc.vector.memset(xpad[:], 0.0)
            nc.vector.memset(square_sb[:], -0.75)
            nc.vector.memset(eps_sb[:], EPS).then_inc(s_setup, 1)
            dve.wait_ge(s_setup, 1)
            dve.wait_ge(s_first, 16 * NFIRST)
            for m in range(2):
                for b in range(2):
                    TT(hT[b][m][:, :, 0], cls_sb[:, m:m + 1].to_broadcast([128, G]),
                       pos_sb[:, m, 0:1].to_broadcast([128, G]), ALU.add)
                last = TS(pos_sb[:, m, 1:], pos_sb[:, m, 1:], bp_sb[:, m:m + 1], None, ALU.add)
            last.then_inc(s_setup, 1)
            for k in range(NA):
                nc.vector.memset(abar[k][:], 0.0)
            nc.vector.memset(mpad[:], 0.0)
            for b in range(2):
                nc.vector.memset(h1[b][:], 0.0)
            nc.vector.memset(va[:], 1.0).then_inc(s_setup, 1)
            dve.wait_ge(s_setup, 3)
            nc.vector.memset(va[0:1, 1:NTILE:2, :, :], 0.0)
            for b in range(2):
                nc.vector.memset(h1[b][:, :, EMB:EMB + 1], 1.0)
            dve.wait_ge(s_load, 16 * NLOADS)
            nc.vector.tensor_copy(sel_sb[:], sel_f32[:])
            dve.wait_ge(s_cast, 1)
            TS(negA[:], negA[:], -1.0, None, ALU.mult).then_inc(s_setup, 1)
            dve.wait_ge(s_setup, 4)

            def term(p, n):
                if n == 0:
                    dve.wait_ge(front_pool, f_pool.count(p, "dtx"))
                dve.wait_ge(b_broadcast, b_done.count(p, n))
                if n >= NU:
                    dve.wait_ge(state_summed, n_done.count(p, n - NU))
                else:
                    if p.has(-1):
                        dve.wait_ge(state_summed, n_done.count(p.plus(-1), NST + n - NU))
                bb = PS[:, BB + n % NBC:BB + n % NBC + 1, 0:T].to_broadcast([128, DC, T])
                TT(state[n % NU][:], dtx[p.parity][:], bb, ALU.mult).then_inc(input_term, u_done.step(n))

            def times_c(p, n):
                dve.wait_ge(c_broadcast, c_done.count(p, n))
                dve.wait_ge(scanned, h_done.count(p, n))
                cb = PS[:, CB + n % NBC:CB + n % NBC + 1, 0:T].to_broadcast([128, DC, T])
                TT(state[n % NU][:], state[n % NU][:], cb, ALU.mult).then_inc(c_applied, hc_done.step(n))

            def scan(p, n):
                dve.wait_ge(decayed, a_done.count(p, n))
                term_done, count = term_read(p, n)
                dve.wait_ge(term_done, count)
                nc.vector.tensor_tensor_scan(
                    flat(state[n % NU]), abar[n % NA][:].rearrange("p c g t -> p (c g t)"), flat(state[n % NU]),
                    0.0, ALU.mult, ALU.add).then_inc(scanned, h_done.step(n))

            def front(f, what):
                b = f.parity
                if what[:5] == "patch":
                    m = int(what[5])
                    dve.wait_ge(front_pe, f_pe.count(f, what))
                    if f.has(-2):
                        dve.wait_ge(attn_pe, a_pe.count(f.plus(-2), "out1"))
                    TT(hT[b][m][:, :, 1:], PS[:, FB, 0:TP].rearrange("p (g t) -> p g t", g=G),
                       pos_sb[:, m:m + 1, 1:].to_broadcast([128, G, NPATCH]),
                       ALU.add).then_inc(front_dve, f_dve.step(f"hT{m}"))
                if what[:4] == "conv":
                    c = int(what[4])
                    dve.wait_ge(front_act, f_act.count(f, f"xz{c}"))
                    if c == 0:
                        if f.has(-1):
                            dve.wait_ge(front_pool, f_pool.count(f.plus(-1), "dt"))
                    acc = cv[:, c, :].rearrange("p (g t) -> p g t", g=G)
                    TS(acc, xpad[:, c, :, 0:LTOK], conv_sb[:, c, 0:1], None, ALU.mult).then_inc(front_dve, f_dve.step(f"conv{c}0"))
                    for j in range(1, NTAP):
                        dve.wait_ge(front_dve, f_dve.count(f, f"conv{c}{j - 1}"))
                        STT(acc, xpad[:, c, :, j:j + LTOK], conv_sb[:, c, j:j + 1], acc,
                                       ALU.mult, ALU.add).then_inc(front_dve, f_dve.step(f"conv{c}{j}"))
                if what == "bc":
                    ps = PS[0:96, FB, 0:T]
                    dve.wait_ge(front_pe, f_pe.count(f, "bc"))
                    nc.vector.tensor_copy(bc[b][:], ps).then_inc(front_dve, f_dve.step("split0"))
                    dve.wait_ge(front_dve, f_dve.count(f, "split0"))
                    TT(bcrest[:], ps[0:64], bc[b][0:64, :], ALU.subtract).then_inc(front_dve, f_dve.step("split1"))
                    dve.wait_ge(front_dve, f_dve.count(f, "split1"))
                    nc.vector.tensor_copy(bc[b][0:64, :], bcrest[:]).then_inc(front_dve, f_dve.step("split2"))
                    dve.wait_ge(front_dve, f_dve.count(f, "split2"))
                    TT(bcrest[0:32, :], bcrest[0:32, :], bc[b][0:32, :], ALU.subtract).then_inc(front_dve, f_dve.step("split3"))
                    dve.wait_ge(front_dve, f_dve.count(f, "split3"))
                    nc.vector.tensor_copy(bc[b][0:32, :], bcrest[0:32, :]).then_inc(front_dve, f_dve.step("split4"))

                if what == "chosen":
                    dve.wait_ge(front_pool, f_pool.count(f, "large"))
                    apart(dve)
                    nc.vector.copy_predicated(flat(dt[b]), flat(ex).bitcast(mybir.dt.uint32), flat(dtx[b])).then_inc(front_dve, f_dve.step("chosen"))

            def attn(a, what):
                b = a.parity
                V = nc.vector

                def norm(k, names, done, order, pe_done, first, second, act_done, deviation, source):
                    s, m = names
                    for t in range(NTILE):
                        if t == 0:
                            dve.wait_ge(pe_done, first)
                        if t == 2:
                            dve.wait_ge(pe_done, second)
                        V.bn_stats(st[k][:, t, :], source(t)).then_inc(done, order.step(f"{s}{t}"))
                    dve.wait_ge(done, order.count(a, f"{s}{NTILE - 1}"))
                    apart(dve)
                    for t in range(NTILE):
                        V.bn_aggr(mv[k][:, t, :], st[k][:, t, :]).then_inc(done, order.step(f"{m}{t}"))
                    dve.wait_ge(done, order.count(a, f"{m}{NTILE - 1}"))
                    dve.wait_ge(act_done, deviation)
                    STT(shift[k][:], mv[k][:, :, 0], -1.0, rs[k][:], ALU.mult, ALU.mult).then_inc(done, order.step("shift"))

                if what == "yz":
                    dve.wait_ge(state_summed, n_done.count(a, NST - 1))
                    if a.has(-1):
                        dve.wait_ge(attn_pe, a_pe.count(a.plus(-1), "out1"))
                    TT(flat(y), flat(yacc), flat(sz[b]), ALU.mult).then_inc(gated, z_done.step("yz"))
                if what == "norm":
                    norm(0, ("st", "mv"), attn_dve, a_dve, attn_pe, a_pe.count(a, "out0"), a_pe.count(a, "out1"),
                         attn_act, a_act.count(a, "ln1"),
                         lambda t: PS[0:ROWS, bank(f"out{t // 2}"), (t % 2) * EMB:(t % 2 + 1) * EMB])
                if what == "gate":
                    lg = PS[0:ROWS, bank("gate"), 0:NTILE * NEXP].rearrange("p (t n) -> p t n", n=NEXP)

                    def wide(v):
                        return v[:].rearrange("p (t o) -> p t o", o=1).to_broadcast([ROWS, NTILE, NEXP])

                    e, pr, cand, oh1, rest = (t[:] for t in gk)
                    dve.wait_ge(attn_pe, a_pe.count(a, "gate"))
                    V.reduce_max(gs[:], lg, AX.X).then_inc(attn_dve, a_dve.step("gmx"))
                    dve.wait_ge(attn_dve, a_dve.count(a, "gmx"))
                    TT(e, lg, wide(gs), ALU.subtract).then_inc(attn_dve, a_dve.step("gd"))
                    dve.wait_ge(attn_act, a_act.count(a, "ge"))
                    V.reduce_sum(gs[:], e, AX.X).then_inc(attn_dve, a_dve.step("gs"))
                    dve.wait_ge(attn_dve, a_dve.count(a, "gs"))
                    V.reciprocal(gs[:], gs[:]).then_inc(attn_dve, a_dve.step("gr"))
                    dve.wait_ge(attn_dve, a_dve.count(a, "gr"))
                    TT(pr, e, wide(gs), ALU.mult).then_inc(attn_dve, a_dve.step("gp"))
                    for k, (src, mark) in enumerate(((pr, "gp"), (rest, "gx"))):
                        dve.wait_ge(attn_dve, a_dve.count(a, mark))
                        V.reduce_max(gs[:], src, AX.X).then_inc(attn_dve, a_dve.step(f"gm{k}"))
                        dve.wait_ge(attn_dve, a_dve.count(a, f"gm{k}"))
                        TT(cand, src, wide(gs), ALU.is_ge).then_inc(attn_dve, a_dve.step(f"ge{k}"))
                        dve.wait_ge(attn_dve, a_dve.count(a, f"ge{k}"))
                        TT(cand, cand, rev_sb[:], ALU.mult).then_inc(attn_dve, a_dve.step(f"gc{k}"))
                        dve.wait_ge(attn_dve, a_dve.count(a, f"gc{k}"))
                        V.reduce_max(gs[:], cand, AX.X).then_inc(attn_dve, a_dve.step(f"gt{k}"))
                        dve.wait_ge(attn_dve, a_dve.count(a, f"gt{k}"))
                        TT(oh1 if k == 0 else cand, cand, wide(gs), ALU.is_equal).then_inc(attn_dve, a_dve.step(f"go{k}"))
                        dve.wait_ge(attn_dve, a_dve.count(a, f"go{k}"))
                        if k == 0:
                            STT(rest, oh1, -2.0, pr, ALU.mult, ALU.add).then_inc(attn_dve, a_dve.step("gx"))
                    TT(oh1, oh1, cand, ALU.add).then_inc(attn_dve, a_dve.step("gu"))
                    dve.wait_ge(attn_dve, a_dve.count(a, "gu"))
                    STT(cand, oh1, float(ALPHA) / RANK, pr, ALU.mult, ALU.mult).then_inc(attn_dve, a_dve.step("gw"))
                    dve.wait_ge(attn_dve, a_dve.count(a, "gw"))
                    wr = wrank.rearrange("p (n r) -> p n r", r=RANK)
                    V.tensor_copy(wr, cand.rearrange("p t (n o) -> p (t n) o", o=1).to_broadcast(
                        [ROWS, NTILE * NEXP, RANK])).then_inc(attn_dve, a_dve.step("gwr"))
                if what == "aw":
                    dve.wait_ge(attn_pe, a_pe.count(a, "spread"))
                    dve.wait_ge(attn_act, a_act.count(a, "down"))
                    TT(aw[:], ad[:], PS[:, bank("spread"), 0:T], ALU.mult).then_inc(attn_dve, a_dve.step("aw"))
                if what[0] == "s" and what[1:].isdigit():
                    k = int(what[1:])
                    g, qt, hp = smax[k]
                    j, i = 2 * hp // QPC, 2 * hp % QPC
                    dve.wait_ge(attn_pe, a_pe.count(a, what))
                    V.reduce_max(
                        mpad[:, 2 * g + qt, 128 * j + MROW + i:128 * j + MROW + i + 2],
                        PS[0:ROWS, bank(what), 0:T].rearrange("p (h t) -> p h t", h=2), AX.X).then_inc(attn_dve, a_dve.step(f"max{k}"))
                if what == "m":
                    for j in range(QC):
                        dve.wait_ge(attn_pe, a_pe.count(a, f"m{j}"))
                        dve.wait_ge(attn_act, a_act.count(a, f"q{j}"))
                        TT(q[:, j, :], q[:, j, :], PS[:, bank(f"m{j}"), 0:T], ALU.add).then_inc(attn_dve, a_dve.step(f"qm{j}"))
                if what == "res":
                    for k in range(2):
                        dve.wait_ge(end_pe, z_pe.count(a, f"proj{k}"))
                        TT(fin[:, 2 * k:2 * k + 2, :],
                           PS[0:ROWS, bank(f"proj{k}"), 0:2 * EMB].rearrange("p (t e) -> p t e", e=EMB),
                           h1[b][:, 2 * k:2 * k + 2, 0:EMB], ALU.add).then_inc(end_dve, z_dve.step(f"res{k}"))
                if what == "fin":
                    norm(1, ("ft", "fv"), end_dve, z_dve, end_dve, z_dve.count(a, "res0"), z_dve.count(a, "res1"),
                         end_act, z_act.count(a, "ln3"), lambda t: fin[:, t, :])

            def part(f, s, a, z):
                if s:
                    term(s, 0)
                for n in steps:
                    if s and n + 1 < NST and n + 1 not in POOL_TERMS:
                        term(s, n + 1)
                    for w, p in works(dve_plan, n, f, a, z):
                        (front if p is f else attn)(p, w)
                    if s and n >= 1:
                        times_c(s, n - 1)
                    for w, p in works(dve_plan, n + 0.3, f, a, z):
                        (front if p is f else attn)(p, w)
                    if s:
                        scan(s, n)
                    for w, p in works(dve_plan, n + 0.6, f, a, z):
                        (front if p is f else attn)(p, w)
                if s:
                    times_c(s, NST - 1)

            program(dve, None, part)

        @block.tensor
        def _(pe):
            MM = nc.tensor.matmul
            pe.wait_ge(s_first, 16 * NFIRST)
            pe.wait_ge(s_setup, 2)

            def b_row(p, n):
                if n == 0:
                    pe.wait_ge(front_dve, f_dve.count(p, "split4"))
                if n >= NBC:
                    reader, count = b_read(p, n - NBC)
                    pe.wait_ge(reader, count)
                elif p.has(-1):
                    reader, count = b_read(p.plus(-1), NST + n - NBC)
                    pe.wait_ge(reader, count)
                MM(PS[:, BB + n % NBC, 0:T], sel_sb[:, n:n + 1].to_broadcast([96, 128]), bc[p.parity][:],
                   start=True, stop=True).then_inc(b_broadcast, b_done.step(n))

            def c_row(p, n):
                if n >= NBC:
                    pe.wait_ge(c_applied, hc_done.count(p, n - NBC))
                elif p.has(-1):
                    pe.wait_ge(c_applied, hc_done.count(p.plus(-1), NST + n - NBC))
                MM(PS[:, CB + n % NBC, 0:T], sel_sb[:, NST + n:NST + n + 1].to_broadcast([96, 128]), bc[p.parity][:],
                   start=True, stop=True).then_inc(c_broadcast, c_done.step(n))

            def front(f, what):
                b = f.parity
                if what == "patch0":
                    pe.wait_ge(s_x, f.times(16, 16))
                    if f.has(-1):
                        pe.wait_ge(front_dve, f_dve.count(f.plus(-1), "split1"))
                if what == "patch1":
                    pe.wait_ge(front_dve, f_dve.count(f, "hT0"))
                if what == "patch0":
                    for k in range(KP):
                        last = MM(PS[:, FB, 0:TP], wpatch_sb[:, k, 0:128], xin[:, k, :],
                                  start=(k == 0), stop=(k == KP - 1))
                    last.then_inc(front_pe, f_pe.step(what))
                if what == "patch1":
                    for k in range(KP // 2):
                        for half in range(2):
                            last = MM(PS[64 * half:64 * half + 64, FB, 0:TP],
                                      wpatch_sb[:, k + KP // 2 * half, 128:EMB], xin[:, k + KP // 2 * half, :],
                                      start=(k == 0), stop=(k == KP // 2 - 1))
                    last.then_inc(front_pe, f_pe.step(what))
                if what[:2] == "xz":
                    m = int(what[2])
                    if m == 0:
                        pe.wait_ge(front_dve, f_dve.count(f, "hT1"))
                    else:
                        pe.wait_ge(front_act, f_act.count(f, f"xz{m - 1}"))
                    MM(PS[:, FB, 0:T], win_sb[:, 0, 128 * m:128 * m + 128], tok(hT[b][0]), start=True, stop=False)
                    MM(PS[:, FB, 0:T], win_sb[:, 1, 128 * m:128 * m + 128], tok(hT[b][1]),
                                 start=False, stop=True).then_inc(front_pe, f_pe.step(what))
                if what == "raw" and f.j is None and f.off == 0:
                    pe.wait_ge(s_setup, 4)
                if what in ("raw", "bc"):
                    pe.wait_ge(front_act, f_act.count(f, "xs" if what == "raw" else f"relu{DC - 1}"))
                    rows = 128 if what == "raw" else 96
                    for c in range(DC):
                        w = wraw_sb[:, c, :].to_broadcast([128, 128]) if what == "raw" else wbc_sb[:, c, :]
                        last = MM(PS[0:rows, FB, 0:T], w, xs[b][:, c, :], start=(c == 0), stop=(c == DC - 1))
                    last.then_inc(front_pe, f_pe.step(what))

            def attn(a, what):
                b = a.parity
                if what[:3] == "out":
                    reader, count = last_read(a, what)
                    if count is not None:
                        pe.wait_ge(reader, count)
                    pe.wait_ge(gated, z_done.count(a, "yz"))
                    for t in (2 * int(what[3]), 2 * int(what[3]) + 1):
                        dst = PS[0:ROWS, bank(what), (t % 2) * EMB:(t % 2 + 1) * EMB]
                        for j in range(DC):
                            MM(dst, y[:, j, cols(t)], wout_sb[:, j, :], start=(j == 0), stop=False)
                        MM(dst, tok(hT[b][0])[:, cols(t)], res0_sb[:], start=False, stop=False)
                        last = MM(dst, tok(hT[b][1])[:, cols(t)], res1_sb[:], start=False, stop=True)
                    last.then_inc(attn_pe, a_pe.step(what))
                if what == "proj":
                    for k in range(2):
                        reader, count = last_read(a.plus(1), f"proj{k}")
                        if count is not None:
                            pe.wait_ge(reader, count)
                        pe.wait_ge(end_pool, z_pool.count(a, "on"))
                        for t in (2 * k, 2 * k + 1):
                            dst = PS[0:ROWS, bank(f"proj{k}"), (t % 2) * EMB:(t % 2 + 1) * EMB]
                            for j in range(HC):
                                last = MM(dst, o[:, j, cols(t)], wo_sb[:, j, :], start=(j == 0), stop=(j == HC - 1))
                        last.then_inc(end_pe, z_pe.step(f"proj{k}"))
                if what == "h1T":
                    for m in range(2):
                        reader, count = last_read(a, f"h1T{m}")
                        if count is not None:
                            pe.wait_ge(reader, count)
                        for t in range(NTILE):
                            pe.wait_ge(attn_act, a_act.count(a, f"norm{t}"))
                            last = nc.tensor.transpose(PS[:, bank(f"h1T{m}"), cols(t)], h1[b][:, t, 128 * m:128 * m + 128],
                                                       id_sb[0:ROWS, 0:ROWS])
                        last.then_inc(attn_pe, a_pe.step(f"h1T{m}"))
                if what == "gate":
                    reader, count = last_read(a, "gate")
                    if count is not None:
                        pe.wait_ge(reader, count)
                    pe.wait_ge(attn_act, a_act.count(a, "h1T1"))
                    for t in range(NTILE):
                        dst = PS[0:ROWS, bank("gate"), NEXP * t:NEXP * t + NEXP]
                        MM(dst, h1T[0][:, cols(t)], wgate_sb[:, 0, :], start=True, stop=False)
                        last = MM(dst, h1T[1][0:65, cols(t)], wgate_sb[0:65, 1, :], start=False, stop=True)
                    last.then_inc(attn_pe, a_pe.step("gate"))
                    reader, count = last_read(a, "down")
                    if count is not None:
                        pe.wait_ge(reader, count)
                    MM(PS[:, bank("down"), 0:T], wdown_sb[:, 0, :], h1T[0][:], start=True, stop=False)
                    MM(PS[:, bank("down"), 0:T], wdown_sb[0:65, 1, :], h1T[1][0:65, :], start=False,
                                 stop=True).then_inc(attn_pe, a_pe.step("down"))
                if what == "spread":
                    reader, count = last_read(a, "spread")
                    if count is not None:
                        pe.wait_ge(reader, count)
                    pe.wait_ge(attn_dve, a_dve.count(a, "gwr"))
                    for t in range(NTILE):
                        last = MM(PS[:, bank("spread"), cols(t)], wrank[:, t * 128:(t + 1) * 128], id_sb[0:ROWS, 0:ROWS], start=True, stop=True)
                    last.then_inc(attn_pe, a_pe.step("spread"))
                if what == "v":
                    pe.wait_ge(attn_dve, a_dve.count(a, "aw"))
                    for k in range(2):
                        reader, count = last_read(a, f"v{k}")
                        if count is not None:
                            pe.wait_ge(reader, count)
                        for t in (2 * k, 2 * k + 1):
                            dst = PS[0:ROWS, bank(f"v{k}"), (t % 2) * EMB:(t % 2 + 1) * EMB]
                            MM(dst, h1T[0][:, cols(t)], wv_sb[:, 0, :], start=True, stop=False)
                            MM(dst, h1T[1][0:65, cols(t)], wv_sb[0:65, 1, :], start=False, stop=False)
                            last = MM(dst, aw[:, cols(t)], wv_sb[:, 2, :], start=False, stop=True)
                        last.then_inc(attn_pe, a_pe.step(f"v{k}"))
                if what[0] in "kq" and len(what) == 2:
                    m = int(what[1]) + (QC if what[0] == "k" else 0)
                    reader, count = last_read(a, what)
                    if count is not None:
                        pe.wait_ge(reader, count)
                    dst = PS[:, bank(what), 0:T]
                    w = slice(128 * m, 128 * m + 128)
                    MM(dst, wqk_sb[:, 0, w], h1T[0][:], start=True, stop=False)
                    MM(dst, wqk_sb[0:65, 1, w], h1T[1][0:65, :], start=False, stop=False)
                    MM(dst, wqk_sb[:, 2, w], aw[:], start=False, stop=True).then_inc(attn_pe, a_pe.step(what))
                if what[0] == "s" and what[1:].isdigit():
                    k = int(what[1:])
                    g, qt, hp = smax[k]
                    j = 2 * hp // QPC
                    reader, count = last_read(a, what)
                    if count is not None:
                        pe.wait_ge(reader, count)
                    pe.wait_ge(attn_act, a_act.count(a, f"q{j}"))
                    for i in range(2):
                        h = 2 * hp + i
                        last = MM(PS[0:ROWS, bank(what), i * LTOK:(i + 1) * LTOK], q[:, j, cols(2 * g + qt)],
                                  km[:, h, g * LTOK:(g + 1) * LTOK], start=True, stop=True)
                    last.then_inc(attn_pe, a_pe.step(what))
                if what == "m":
                    for j in range(QC):
                        reader, count = last_read(a, f"m{j}")
                        if count is not None:
                            pe.wait_ge(reader, count)
                        pe.wait_ge(attn_dve, a_dve.count(a, f"max{len(smax) - 1}"))
                        for t in range(NTILE):
                            last = nc.tensor.transpose(PS[:, bank(f"m{j}"), cols(t)], mpad[:, t, 128 * j:128 * j + 128],
                                                       id_sb[0:ROWS, 0:ROWS])
                        last.then_inc(attn_pe, a_pe.step(f"m{j}"))
                if what[0] == "t":
                    k, kt, hp = (int(c) for c in what[1:])
                    g, j = groups[k]
                    reader, count = last_read(a, what)
                    if count is not None:
                        pe.wait_ge(reader, count)
                    pe.wait_ge(attn_dve, a_dve.count(a, f"qm{QC - 1}"))
                    for i in range(2):
                        h = j * HPC + 2 * hp + i
                        last = MM(PS[0:ROWS, bank(what), i * LTOK:(i + 1) * LTOK], km[:, h, cols(2 * g + kt)],
                                  q[:, h // QPC, g * LTOK:(g + 1) * LTOK], start=True, stop=True)
                    last.then_inc(attn_pe, a_pe.step(what))
                if what[:2] == "pv":
                    k = int(what[2])
                    g, j = groups[k]
                    reader, count = last_read(a, what)
                    if count is not None:
                        pe.wait_ge(reader, count)
                    pe.wait_ge(attn_act, a_act.count(a, f"e{k}11"))
                    for kt in range(2):
                        for i in range(HPC):
                            last = MM(PS[HSLOT * i:HSLOT * (i + 1), bank(what), 0:LTOK],
                                      va[:, 2 * g + kt, j * HPC + i, :], pT[k % 2][:, kt, i, :],
                                      start=(kt == 0), stop=(kt == 1))
                    last.then_inc(attn_pe, a_pe.step(what))
                if what == "r":
                    for j in range(HC):
                        reader, count = last_read(a, f"r{j}")
                        if count is not None:
                            pe.wait_ge(reader, count)
                        pe.wait_ge(attn_act, a_act.count(a, f"o{len(groups) - 1}"))
                        MM(PS[:, bank(f"r{j}"), 0:T], swap_sb[:], o[:, j, :], start=True, stop=True).then_inc(attn_pe, a_pe.step(f"r{j}"))

            def part(f, s, a, z):
                if s:
                    b_row(s, 0)
                    b_row(s, 1)
                for n in steps:
                    if s:
                        if n + 2 < NST:
                            b_row(s, n + 2)
                        c_row(s, n)
                    for w, p in works(pe_plan, n, f, a, z):
                        (front if p is f else attn)(p, w)

            program(pe, None, part)


_NAMES = ["x", "w_patch", "pos", "cls", "b_patch", "w_in", "w_conv", "w_proj_bc", "w_proj_dt", "w_dt", "b_dt",
          "a_log", "d_param", "w_out", "w_qk", "w_v", "w_gate", "w_down", "w_o", "res0", "res1",
          "ident", "swap", "sel", "kmask", "vmask", "rev"]


def lay_out(np, i):
    f = {k: np.ascontiguousarray(v) for k, v in i.items()}

    def chunks(w, bias=None):
        k, n = w.shape
        kc = -(-k // 128)
        a = np.zeros((kc * 128, n), np.float32)
        a[:k] = w
        if bias is not None:
            a[k] = bias
        return np.ascontiguousarray(a.reshape(kc, 128, n).transpose(1, 0, 2))

    d = {}
    v = f["x"].reshape(NPAIR, G, SIDE, PATCH, SIDE, PATCH, CH)
    v = v.transpose(0, 6, 3, 5, 1, 2, 4).reshape(NPAIR, KP, 128, TP)
    d["x"] = np.ascontiguousarray(v.transpose(0, 2, 1, 3))
    d["w_patch"] = chunks(f["L0_tok_W"].T)
    d["pos"] = chunks(f["L0_tok_pos_embed"][0].T)
    d["cls"] = chunks(f["L0_tok_cls_token"].reshape(EMB, 1))[:, :, 0]
    d["b_patch"] = chunks(f["L0_tok_b"].reshape(EMB, 1))[:, :, 0]
    w = f["L0_attn_w_in"].T
    d["w_in"] = chunks(np.concatenate([w, w[128:]]))
    d["w_conv"] = chunks(f["L0_attn_w_conv"].reshape(DIN, NTAP))
    xp = f["L0_attn_w_xproj"]
    d["w_proj_bc"] = chunks(np.concatenate([xp[1:].T] * 3, axis=1))
    d["w_proj_dt"] = chunks(xp[0:1].T)
    d["w_dt"] = chunks(f["L0_attn_w_dt"])[:, :, 0]
    d["b_dt"] = chunks(f["L0_attn_b_dt"].reshape(DIN, 1))[:, :, 0]
    d["a_log"] = chunks(f["L0_attn_a_log"])
    d["d_param"] = chunks(f["L0_attn_d_param"].reshape(DIN, 1))[:, :, 0]
    d["w_out"] = chunks(f["L0_attn_w_out"].T)
    wq, bq = f["L0_ffn_W_qkv"].T, f["L0_ffn_b_qkv"]
    lora = f["L0_ffn_B_lora"].transpose(0, 2, 1).reshape(NEXP * RANK, 3 * EMB)

    def slots(w):
        a = np.zeros((w.shape[0], 2 * QC, 128), np.float32)
        a[:, :, :MROW] = w[:, :2 * EMB].reshape(w.shape[0], 2 * QC, MROW)
        return a

    bqk = slots(bq[None])
    bqk[:, QC:, MROW:MROW + QPC] = -1.0
    d["w_qk"] = np.concatenate([chunks(slots(wq).reshape(EMB, -1), bqk.reshape(-1)),
                                chunks(slots(lora).reshape(NEXP * RANK, -1))], axis=1)
    d["w_v"] = np.concatenate([chunks(wq[:, 2 * EMB:], bq[2 * EMB:]), chunks(lora[:, 2 * EMB:])], axis=1)
    d["w_gate"] = chunks(f["L0_ffn_W_gate"].T, f["L0_ffn_b_gate"])
    d["w_down"] = chunks(f["L0_ffn_A"].reshape(NEXP * RANK, EMB).T)
    wo = np.zeros((HEADS, HSLOT, EMB), np.float32)
    wo[:, :HD] = f["L0_ffn_W_proj"].T.reshape(HEADS, HD, EMB)
    wo[0, HD] = f["L0_ffn_b_proj"]
    d["w_o"] = chunks(wo.reshape(HEADS * HSLOT, EMB))
    eye = np.eye(EMB, dtype=np.float32)
    d["res0"] = eye[:128]
    d["res1"] = np.concatenate([eye[128:], eye[128:]])
    d["ident"] = np.eye(128, dtype=np.float32)
    s = np.zeros((128, 128), np.float32)
    for m in range(128):
        s[m // HSLOT * HSLOT + HD + m % HD, m] = 1.0
    d["swap"] = s
    d["sel"] = np.concatenate([np.eye(2 * NST, dtype=np.float32)] * 3)
    km = np.zeros((128, QPC), np.float32)
    for i in range(QPC):
        km[HD * i:HD * i + HD, i] = km[MROW + i, i] = 1.0
    d["kmask"] = km
    vm = np.ones((ROWS, 1), np.float32)
    vm[0] = 0.0
    d["vmask"] = vm
    d["rev"] = np.broadcast_to(np.arange(NEXP, 0, -1, dtype=np.float32), (ROWS, NTILE, NEXP))
    return {k: np.ascontiguousarray(d[k]) for k in _NAMES}


def kernel(**inputs):
    import numpy as _np
    import concourse.bacc as _bacc
    from concourse import mybir as _mybir
    from concourse.bass_utils import run_bass_kernel_spmd as _run

    nc = _bacc.Bacc("TRN2", target_bir_lowering=False, num_devices=1)
    laid = lay_out(_np, {k: _np.asarray(v) for k, v in inputs.items()})
    arrays, args = {}, []
    for name, a in laid.items():
        arrays[f"in_{name}_dram"] = a
        args.append(nc.dram_tensor(f"in_{name}_dram", a.shape, _mybir.dt.from_np(a.dtype), kind="ExternalInput").ap())
    args.append(nc.dram_tensor("out_0_dram", (NPAIR, G, LTOK, EMB), _mybir.dt.float32, kind="ExternalOutput").ap())
    tower_kernel(nc, *args)
    r = _run(nc, [arrays], core_ids=[0])
    return r.results[0]["out_0_dram"].reshape(NB, LTOK, EMB)
```
